# Optimizing a Trainium2 kernel written in Bass

```python
import numpy as np
import jax
import jax.numpy as jnp

def _softmax(x, axis=-1):
    return jax.nn.softmax(x, axis=axis)
def _gelu(x):
    return jax.nn.gelu(x, approximate=True)
def _silu(x):
    return jax.nn.silu(x)
def _sigmoid(x):
    return jax.nn.sigmoid(x)
def _layernorm(x, axis=-1, eps=1e-5):
    m = jnp.mean(x, axis=axis, keepdims=True)
    v = jnp.var(x, axis=axis, keepdims=True)
    return (x - m) / jnp.sqrt(v + eps)
def _scatter_add(tgt, idx, src, axis=0):
    return tgt.at[idx].add(src)
def _segment_sum(src, seg, n):
    return jax.ops.segment_sum(src, seg, n)

kernel_name = 'mk_adj_resnorm_d2_adj_128_313080'

def setup_inputs(seed: int = 0):
    np.random.seed(seed)
    _w = jnp.asarray
    def _rec_inputs():
        import jax
        import jax.numpy as jnp
        _gk = jax.random.key(seed)
        x = -0.000929 + 1 * jax.random.normal(jax.random.fold_in(_gk, 1), (8192, 128), jnp.float32)
        _a = jax.random.bernoulli(jax.random.fold_in(_gk, 2), 0.000488281, (8192, 8192))
        _a = jnp.logical_or(_a, jnp.swapaxes(_a, -1, -2))
        _a = jnp.logical_or(_a, jnp.eye(8192, dtype=bool))
        _af = _a.astype(jnp.float32)
        _af = _af * jax.random.uniform(jax.random.fold_in(_gk, 3), (8192, 8192), jnp.float32, 0.05, 0.0598829)
        adj = _af
        return x, adj
    x, adj = _rec_inputs()
    def _L0_gnn_setup():
        import jax, jax.numpy as jnp
        import numpy as np
        V0, V1, C = (64, 128, 128)
        V = V0 * V1
        key = jax.random.key(seed)
        ks = jax.random.split(key, 8)
        x = jax.random.normal(ks[0], (V, C), dtype=jnp.float32)
        edge_index = jax.random.randint(ks[1], (2, 100), 0, V)
        L = jnp.zeros((2, 2), dtype=jnp.float32)
        mass = jax.random.uniform(ks[2], (V,), dtype=jnp.float32) + 0.5
        evals0 = jax.random.uniform(ks[3], (V0,), dtype=jnp.float32) * 2.0
        evals1 = jax.random.uniform(ks[4], (V1,), dtype=jnp.float32) * 2.0
        evecs = jax.random.normal(ks[5], (V, V), dtype=jnp.float32) / np.float32(np.sqrt(V))
        diffusion_time = jax.random.uniform(ks[6], (2, C), dtype=jnp.float32)
        return {'x': x, 'edge_index': edge_index, 'L': L, 'mass': mass, 'evals0': evals0, 'evals1': evals1, 'evecs': evecs, 'diffusion_time': diffusion_time}
    _L0_gnn_all = _L0_gnn_setup()
    _L0_gnn_in = {k: v for k, v in _L0_gnn_all.items() if k in ('edge_index', 'L', 'mass', 'evals0', 'evals1', 'diffusion_time', )}
    del _L0_gnn_all

    def _L1_gnn_setup():
        import jax, jax.numpy as jnp
        import numpy as np
        N, IN, H, C = (4096, 128, 4, 32)
        HC = H * C
        EDGE_P = 0.008

        def _linear_params(key, fan_in, fan_out, bias=True):
            k1, k2 = jax.random.split(key)
            lim = 1.0 / np.sqrt(fan_in)
            W = jax.random.uniform(k1, (fan_in, fan_out), jnp.float32, -lim, lim)
            if not bias:
                return W
            b = jax.random.uniform(k2, (fan_out,), jnp.float32, -lim, lim)
            return (W, b)

        def _transformer_conv(x, adj, Wq, bq, Wk, bk, Wv, bv, Ws, bs, Wb):
            n = x.shape[0]
            q = (x @ Wq + bq).reshape(n, H, C)
            k = (x @ Wk + bk).reshape(n, H, C)
            v = (x @ Wv + bv).reshape(n, H, C)
            attn = jnp.einsum('nhc,mhc->hnm', q, k) / np.float32(np.sqrt(C))
            mask = adj == 0.0
            neg = jnp.where(mask[None], -jnp.inf, attn)
            m = jnp.max(neg, axis=-1, keepdims=True)
            all_inf = jnp.isneginf(m)
            e = jnp.where(mask[None], 0.0, jnp.exp(neg - jnp.where(all_inf, 0.0, m)))
            denom = jnp.sum(e, axis=-1, keepdims=True)
            alpha = e / jnp.where(denom == 0.0, 1.0, denom)
            out = jnp.einsum('hnm,mhc->hnc', alpha, v)
            out = jnp.transpose(out, (1, 2, 0)).reshape(n, C * H)
            x_r = x @ Ws + bs
            beta = jax.nn.sigmoid(jnp.concatenate([out, x_r, out - x_r], axis=-1) @ Wb)
            return beta * x_r + (1.0 - beta) * out
        key = jax.random.key(seed)
        ks = jax.random.split(key, 7)
        x = jax.random.normal(ks[0], (N, IN), jnp.float32)
        adj = (jax.random.uniform(ks[1], (N, N)) < EDGE_P).astype(jnp.float32)
        Wq, bq = _linear_params(ks[2], IN, HC)
        Wk, bk = _linear_params(ks[3], IN, HC)
        Wv, bv = _linear_params(ks[4], IN, HC)
        Ws, bs = _linear_params(ks[5], IN, HC)
        Wb = _linear_params(ks[6], 3 * HC, 1, bias=False)
        return dict(x=x, adj=adj, Wq=Wq, bq=bq, Wk=Wk, bk=bk, Wv=Wv, bv=bv, Ws=Ws, bs=bs, Wb=Wb)
    _L1_gnn_all = _L1_gnn_setup()
    _L1_gnn_in = {k: v for k, v in _L1_gnn_all.items() if k in ('Wq', 'bq', 'Wk', 'bk', 'Wv', 'bv', 'Ws', 'bs', 'Wb', )}
    del _L1_gnn_all

    return {
        "x": x,
        "adj": adj,
        "L0_gnn_edge_index": _L0_gnn_in["edge_index"],
        "L0_gnn_L": _L0_gnn_in["L"],
        "L0_gnn_mass": _L0_gnn_in["mass"],
        "L0_gnn_evals0": _L0_gnn_in["evals0"],
        "L0_gnn_evals1": _L0_gnn_in["evals1"],
        "L0_gnn_diffusion_time": _L0_gnn_in["diffusion_time"],
        "L1_gnn_Wq": _L1_gnn_in["Wq"],
        "L1_gnn_bq": _L1_gnn_in["bq"],
        "L1_gnn_Wk": _L1_gnn_in["Wk"],
        "L1_gnn_bk": _L1_gnn_in["bk"],
        "L1_gnn_Wv": _L1_gnn_in["Wv"],
        "L1_gnn_bv": _L1_gnn_in["bv"],
        "L1_gnn_Ws": _L1_gnn_in["Ws"],
        "L1_gnn_bs": _L1_gnn_in["bs"],
        "L1_gnn_Wb": _L1_gnn_in["Wb"],
    }

def reference(x, adj, L0_gnn_edge_index, L0_gnn_L, L0_gnn_mass, L0_gnn_evals0, L0_gnn_evals1, L0_gnn_diffusion_time, L1_gnn_Wq, L1_gnn_bq, L1_gnn_Wk, L1_gnn_bk, L1_gnn_Wv, L1_gnn_bv, L1_gnn_Ws, L1_gnn_bs, L1_gnn_Wb):
    import jax
    import jax.numpy as jnp
    def _L0_gnn_ref(x, edge_index, L, mass, evals0, evals1, evecs, diffusion_time):
        import jax, jax.numpy as jnp
        import numpy as np
        V0, V1, C = (64, 128, 128)
        V = V0 * V1
        x_spec = evecs.T @ (x * mass[:, None])
        e0 = jnp.exp(-evals0[:, None] * diffusion_time[0][None, :])
        e1 = jnp.exp(-evals1[:, None] * diffusion_time[1][None, :])
        diffusion_coefs = (e0[:, None, :] * e1[None, :, :]).reshape(V0 * V1, C)
        x_diffuse = evecs @ (diffusion_coefs * x_spec)
        return x_diffuse

    def _L1_gnn_ref(x, adj, Wq, bq, Wk, bk, Wv, bv, Ws, bs, Wb):
        import jax, jax.numpy as jnp
        import numpy as np
        N, IN, H, C = (4096, 128, 4, 32)
        HC = H * C
        EDGE_P = 0.008

        def _linear_params(key, fan_in, fan_out, bias=True):
            k1, k2 = jax.random.split(key)
            lim = 1.0 / np.sqrt(fan_in)
            W = jax.random.uniform(k1, (fan_in, fan_out), jnp.float32, -lim, lim)
            if not bias:
                return W
            b = jax.random.uniform(k2, (fan_out,), jnp.float32, -lim, lim)
            return (W, b)

        def _transformer_conv(x, adj, Wq, bq, Wk, bk, Wv, bv, Ws, bs, Wb):
            n = x.shape[0]
            q = (x @ Wq + bq).reshape(n, H, C)
            k = (x @ Wk + bk).reshape(n, H, C)
            v = (x @ Wv + bv).reshape(n, H, C)
            attn = jnp.einsum('nhc,mhc->hnm', q, k) / np.float32(np.sqrt(C))
            mask = adj == 0.0
            neg = jnp.where(mask[None], -jnp.inf, attn)
            m = jnp.max(neg, axis=-1, keepdims=True)
            all_inf = jnp.isneginf(m)
            e = jnp.where(mask[None], 0.0, jnp.exp(neg - jnp.where(all_inf, 0.0, m)))
            denom = jnp.sum(e, axis=-1, keepdims=True)
            alpha = e / jnp.where(denom == 0.0, 1.0, denom)
            out = jnp.einsum('hnm,mhc->hnc', alpha, v)
            out = jnp.transpose(out, (1, 2, 0)).reshape(n, C * H)
            x_r = x @ Ws + bs
            beta = jax.nn.sigmoid(jnp.concatenate([out, x_r, out - x_r], axis=-1) @ Wb)
            return beta * x_r + (1.0 - beta) * out
        return _transformer_conv(x, adj, Wq, bq, Wk, bk, Wv, bv, Ws, bs, Wb)

    x = _layernorm(x + _L0_gnn_ref(x, L0_gnn_edge_index, L0_gnn_L, L0_gnn_mass, L0_gnn_evals0, L0_gnn_evals1, adj, L0_gnn_diffusion_time), axis=-1)
    x = _layernorm(x + _L1_gnn_ref(x, adj, L1_gnn_Wq, L1_gnn_bq, L1_gnn_Wk, L1_gnn_bk, L1_gnn_Wv, L1_gnn_bv, L1_gnn_Ws, L1_gnn_bs, L1_gnn_Wb), axis=-1)
    return x


_drawn_inputs = setup_inputs


def setup_inputs(seed=0):
    import zlib

    import numpy as np

    out = dict(_drawn_inputs(seed))
    spreads = {'L0_gnn_L': (0.0, 0.1)}
    factors = {'L0_gnn_mass': 200.0,
     'L0_gnn_evals0': 200.0,
     'L0_gnn_evals1': 200.0,
     'L0_gnn_diffusion_time': 200.0,
     'L1_gnn_bq': 8.0,
     'L1_gnn_bk': 200.0}
    for name, (base, spread) in spreads.items():
        noise = np.random.default_rng([zlib.crc32(name.encode()), seed]).standard_normal(out[name].shape)
        drawn = base * np.exp(spread * noise) if base else spread * noise
        out[name] = jnp.asarray(drawn.astype(out[name].dtype))
    for name, factor in factors.items():
        out[name] = (out[name] * factor).astype(out[name].dtype)
    return out
```

```python
from contextlib import ExitStack

import numpy as np

import concourse.bass as bass
from concourse import mybir

F32 = mybir.dt.float32
ALU = mybir.AluOpType
ACT = mybir.ActivationFunctionType
AX_X = mybir.AxisListType.X

P = 128
N = 8192
C = 128
T = N // P
V0, V1 = 64, 128
H, HC = 4, 32
BANK = 512
HALF = N // 2
NBUF = 4
EPS = 1e-5
SCALE = float(1.0 / np.sqrt(np.float32(HC)))
CREDIT = 1
FAR = 1e30


class Steps:

    def __init__(self, eng, sem):
        self.eng, self.sem, self.base, self.turn, self.k = eng, sem, 0, None, 0

    def __call__(self, ins):
        self.k += 1
        ins.then_inc(self.sem, 1)
        past = self.base if self.turn is None else self.turn * self.per + self.base
        self.eng.wait_ge(self.sem, past + self.k)

    def enter(self, turn, per):
        self.base += self.k
        self.turn, self.per, self.k = turn, per, 0

    def leave(self, turns):
        assert self.k == self.per, (self.k, self.per)
        self.base += turns * self.per
        self.turn, self.k = None, 0


def build_program(nc, x, adj, mass, evals0, evals1, diff_time, Wq, bq, Wk, bk, Wv, bv, Ws, bs, Wb, out):
    with ExitStack() as ctx:
        def sb(name, shape, dt=F32):
            return ctx.enter_context(nc.sbuf_tensor(name, shape, dt))

        def sem(name):
            return ctx.enter_context(nc.semaphore(name))

        keep = nc.dram_tensor("kept_rows", [N, 2 * C], F32, kind="Internal").ap()

        arena = sb("arena", [P, 5 * N])
        region = [arena[:, r * N:(r + 1) * N] for r in range(5)]
        yT, kT = region[0], region[0]
        y_rows = region[1].rearrange("p (t c) -> p t c", c=C)
        scores = region[1]
        x_rows = region[2].rearrange("p (t c) -> p t c", c=C)
        v_rows = region[2].rearrange("p (t c) -> p t c", c=C)
        adj_buf = [arena[:, 3 * N + b * HALF:3 * N + (b + 1) * HALF] for b in range(NBUF)]
        qT = region[4]

        ident = sb("ident", [P, P])
        mass_sb = sb("mass_sb", [P, T])
        time_col = sb("time_col", [P, 2])
        neg_time = sb("neg_time", [P, 2])
        ev0 = sb("ev0", [P, V0])
        ev1 = sb("ev1", [P, V1])
        decay0 = sb("decay0", [P, V0])
        decay1 = sb("decay1", [P, V1])
        W_all = sb("W_all", [P, 4 * C])
        bq_col = sb("bq_col", [P, 1])
        bk_col = sb("bk_col", [P, 1])
        b_vs = sb("b_vs", [P, 2 * C])
        Wb_rows = sb("Wb_rows", [P, 3 * C])
        xm = [sb(f"xm{b}", [P, C]) for b in range(NBUF)]
        minus_half = sb("minus_half", [P, 1])
        turned = [sb(f"turned{b}", [P, BANK]) for b in range(2)]
        x_tile = sb("x_tile", [P, C])
        pre = sb("pre", [P, C])
        kept = sb("kept", [P, 2 * C])
        x1T = sb("x1T", [P, C])
        centred = sb("centred", [P, C])
        squares = sb("squares", [P, C])
        moments = sb("moments", [P, 2])
        rstd = sb("rstd", [P, 1])
        qz = sb("qz", [P, H, P])
        rowmax = sb("rowmax", [P, H])
        shift = sb("shift", [P, H])
        den = sb("den", [P, H])
        inv = sb("inv", [P, H])
        cat = sb("cat", [P, 3 * C])
        prod = sb("prod", [P, 3 * C])
        beta = sb("beta", [P, 4])
        res = sb("res", [P, C])
        kept_in = sb("kept_in", [P, 2 * C])

        bank = [ctx.enter_context(nc.psum_tensor(f"bank{b}", [P, BANK], F32)) for b in range(8)]

        loaded = sem("loaded")
        ident_ready = sem("ident_ready")
        adj_landed = [sem(f"adj_landed{b}") for b in range(NBUF)]
        xm_ready = sem("xm_ready")
        adj_summed = sem("adj_summed")
        decay_ready = sem("decay_ready")
        neg_ready = sem("neg_ready")
        y_scaled = sem("y_scaled")
        y_turned = [sem(f"y_turned{b}") for b in range(2)]
        y_copied = [sem(f"y_copied{b}") for b in range(2)]
        dve_step = sem("dve_step")
        block_landed = [sem(f"block_landed{b}") for b in range(2)]
        x_landed = sem("x_landed")
        turned_psum = [sem(f"turned_psum{b}") for b in range(2)]
        turned_sbuf = [sem(f"turned_sbuf{b}") for b in range(2)]
        turned_used = [sem(f"turned_used{b}") for b in range(2)]
        var_ready = sem("var_ready")
        rstd_ready = sem("rstd_ready")
        x1_ready = sem("x1_ready")
        x1T_psum = sem("x1T_psum")
        x1T_ready = sem("x1T_ready")
        proj_ready = sem("proj_ready")
        kept_ready = sem("kept_ready")
        kept_stored = sem("kept_stored")
        kept_back = sem("kept_back")
        q_ready = sem("q_ready")
        s_psum = [sem(f"s_psum{b}") for b in range(2)]
        s_masked = [sem(f"s_masked{b}") for b in range(2)]
        shift_ready = sem("shift_ready")
        exp_ready = sem("exp_ready")
        p_psum = [sem(f"p_psum{b}") for b in range(2)]
        p_sbuf = [sem(f"p_sbuf{b}") for b in range(2)]
        p_used = [sem(f"p_used{b}") for b in range(2)]
        head_ready = sem("head_ready")
        head_used = sem("head_used")
        inv_ready = sem("inv_ready")
        logit_ready = sem("logit_ready")
        beta_ready = sem("beta_ready")
        var2_ready = sem("var2_ready")
        rstd2_ready = sem("rstd2_ready")
        res_ready = sem("res_ready")
        res_stored = sem("res_stored")
        N_CONST = 14

        block = ctx.enter_context(nc.Block())

        @block.sync
        def _(sp):
            for to, of in (
                (x_rows, x.rearrange("(t p) c -> p t c", p=P)),
                (mass_sb[:], mass),
                (time_col[:], diff_time),
                (ev0[:], evals0.partition_broadcast(P)),
                (ev1[:], evals1.partition_broadcast(P)),
                (W_all[:, 0:C], Wq), (W_all[:, C:2 * C], Wk),
                (W_all[:, 2 * C:3 * C], Wv), (W_all[:, 3 * C:], Ws),
                (bq_col[:], bq), (bk_col[:], bk),
                (b_vs[:, 0:C], bv.partition_broadcast(P)), (b_vs[:, C:], bs.partition_broadcast(P)),
                (Wb_rows[:], Wb.rearrange("c a -> (a c)").partition_broadcast(P)),
            ):
                sp.dma_start(to, of).then_inc(loaded, 16)

            def load_block(h, g, b):
                rows = bass.ds((g * NBUF + b) * P, P)
                sp.dma_start(adj_buf[b], adj[rows, h * HALF:(h + 1) * HALF]).then_inc(adj_landed[b], 16)

            for b in range(NBUF):
                load_block(0, 0, b)
            for h in range(2):
                with sp.Fori(1 - h, T // NBUF) as g:
                    for b in range(NBUF):
                        sp.wait_ge(adj_summed, h * T + g * NBUF + (b + 1 - NBUF))
                        load_block(h, g, b)

            sp.wait_ge(adj_summed, 2 * T)
            with sp.Fori(0, T) as t:
                for half in range(2):
                    sp.wait_ge(turned_psum[1], (t * 8 + 4 * half - 4 if half else t * 8) + CREDIT)
                    sp.dma_start(adj_buf[half], adj[bass.ds(t * P, P), half * HALF:(half + 1) * HALF])\
                      .then_inc(block_landed[half], 16)
                sp.wait_ge(x1_ready, t + CREDIT)
                sp.dma_start(x_tile[:], x[bass.ds(t * P, P), :]).then_inc(x_landed, 16)
                sp.wait_ge(kept_ready, t + 1 + CREDIT)
                sp.dma_start(keep[bass.ds(t * P, P), :], kept[:]).then_inc(kept_stored, 16)
            sp.wait_ge(kept_stored, 16 * T + CREDIT)
            with sp.Fori(0, T) as t:
                sp.wait_ge(s_masked[0], t * (H * 8) + CREDIT)
                sp.wait_ge(s_masked[1], t * (H * 8) + CREDIT)
                for half in range(2):
                    sp.dma_start(adj_buf[half], adj[bass.ds(t * P, P), half * HALF:(half + 1) * HALF])\
                      .then_inc(block_landed[half], 16)
                sp.wait_ge(res_ready, t + CREDIT)
                sp.dma_start(kept_in[:], keep[bass.ds(t * P, P), :]).then_inc(kept_back, 16)
                sp.wait_ge(res_ready, t + 1 + CREDIT)
                sp.dma_start(out[bass.ds(t * P, P), :], res[:]).then_inc(res_stored, 16)
            sp.wait_ge(res_stored, 16 * T + CREDIT)

        @block.gpsimd
        def _(pool):
            for credited in (*turned_psum, *turned_sbuf, *turned_used, x1_ready, kept_ready, kept_stored, *s_masked,
                             res_ready, *p_psum, *p_sbuf, *p_used, head_used, res_stored):
                pool.sem_inc(credited, CREDIT)
            pool.memset(ident[:], 0.0).then_inc(ident_ready, 1)
            pool.memset(minus_half[:], -0.5).then_inc(ident_ready, 1)
            pool.wait_ge(ident_ready, 2)
            pool.affine_select(out=ident[:], in_=ident[:], compare_op=ALU.not_equal, fill=1.0, base=0,
                               pattern=[[-1, P]], channel_multiplier=1).then_inc(ident_ready, 1)
            with pool.Fori(0, T) as t:
                pool.wait_ge(var_ready, t + 1)
                pool.tensor_tensor(rstd[:], moments[:, 1:2], minus_half[:], ALU.pow).then_inc(rstd_ready, 1)
            with pool.Fori(0, T) as t:
                pool.wait_ge(var2_ready, t + 1)
                pool.tensor_tensor(rstd[:], moments[:, 1:2], minus_half[:], ALU.pow).then_inc(rstd2_ready, 1)

        @block.scalar
        def _(act):
            act.wait_ge(neg_ready, 1)
            act.activation(decay0[:], ev0[:], ACT.Exp, scale=neg_time[:, 0:1]).then_inc(decay_ready, 1)
            act.activation(decay1[:], ev1[:], ACT.Exp, scale=neg_time[:, 1:2]).then_inc(decay_ready, 1)

            def weigh(g, b):
                t = g * NBUF + b
                act.activation(xm[b][:], x_rows[:, t, :], ACT.Copy, scale=mass_sb[:, bass.ds(t, 1)])\
                   .then_inc(xm_ready, 1)

            act.wait_ge(loaded, 16 * N_CONST)
            for h in range(2):
                if h == 0:
                    for b in range(NBUF):
                        weigh(0, b)
                with act.Fori(1 - h, T // NBUF) as g:
                    for b in range(NBUF):
                        act.wait_ge(adj_summed, h * T + g * NBUF + (b + 1 - NBUF))
                        weigh(g, b)
            for j in range(1, 16, 2):
                act.wait_ge(y_turned[1], j // 2 + 1)
                act.activation(y_rows[:, 4 * j:4 * j + 4, :].rearrange("p t c -> p (t c)"), bank[1][:], ACT.Copy)\
                   .then_inc(y_copied[1], 1)
            with act.Fori(0, T) as t:
                for j in range(8):
                    act.wait_ge(turned_psum[1], t * 8 + (j + 1) + CREDIT)
                    act.wait_ge(turned_used[1], t * 8 + j + CREDIT)
                    act.activation(turned[1][:], bank[1][:], ACT.Copy).then_inc(turned_sbuf[1], 1)
                act.wait_ge(x1T_psum, t + 1)
                act.activation(x1T[:], bank[4][:, 0:P], ACT.Copy).then_inc(x1T_ready, 1)
            with act.Fori(0, T) as t:
                for h in range(H):
                    act.wait_ge(shift_ready, t * H + (h + 1))
                    act.activation(scores, scores, ACT.Exp, bias=shift[:, h:h + 1],
                                   accum_out=den[:, h:h + 1]).then_inc(exp_ready, 1)
                    for j in range(8):
                        act.wait_ge(p_psum[1], (t * H + h) * 8 + (j + 1) + CREDIT)
                        act.wait_ge(p_used[1], (t * H + h) * 8 + j + CREDIT)
                        act.activation(turned[1][:], bank[1][:], ACT.Copy).then_inc(p_sbuf[1], 1)
                act.wait_ge(logit_ready, t + 1)
                act.activation(beta[:, 1:2], beta[:, 0:1], ACT.Exp, scale=-1.0).then_inc(beta_ready, 1)

        @block.tensor
        def _(pe):
            def add_block(h, g, b, first, last):
                pe.wait_ge(adj_landed[b], g * 16 + 16 * (h * (T // NBUF) + 1))
                pe.wait_ge(xm_ready, g * NBUF + (h * T + b + 1))
                for k in range(8):
                    if h and first:
                        pe.wait_ge(y_scaled, k + 1)
                    mm = pe.matmul(bank[k][:], xm[b][:], adj_buf[b][:, k * BANK:(k + 1) * BANK],
                                   start=first, stop=last)
                mm.then_inc(adj_summed, 1)

            for h in range(2):
                for b in range(NBUF):
                    add_block(h, 0, b, b == 0, False)
                with pe.Fori(1, T // NBUF - 1) as g:
                    for b in range(NBUF):
                        add_block(h, g, b, False, False)
                for b in range(NBUF):
                    add_block(h, T // NBUF - 1, b, False, b == NBUF - 1)
            pe.wait_ge(y_scaled, 16)
            pe.wait_ge(ident_ready, 3)
            for j in range(16):
                if j >= 2:
                    pe.wait_ge(y_copied[j % 2], j // 2)
                for i in range(4):
                    tp = pe.transpose(bank[j % 2][:, i * P:(i + 1) * P], yT[:, (4 * j + i) * P:(4 * j + i + 1) * P],
                                      ident[:])
                tp.then_inc(y_turned[j % 2], 1)
            for p in range(2):
                pe.wait_ge(y_copied[p], 8)

            with pe.Fori(0, T) as t:
                def add_group(j):
                    pe.wait_ge(turned_sbuf[j % 2], t * 8 + (j // 2 + 1) + CREDIT)
                    for i in range(4):
                        m = 4 * j + i
                        mm = pe.matmul(bank[2][:, 0:C], turned[j % 2][:, i * P:(i + 1) * P], y_rows[:, m, :],
                                       start=m == 0, stop=m == T - 1)
                    mm.then_inc(turned_used[j % 2], 1)
                    return mm

                for j in range(16):
                    if j % 8 == 0:
                        pe.wait_ge(block_landed[j // 8], t * 16 + 16)
                    pe.wait_ge(turned_sbuf[j % 2], t * 8 + j // 2 + CREDIT)
                    for i in range(4):
                        k = 4 * (j % 8) + i
                        tp = pe.transpose(bank[j % 2][:, i * P:(i + 1) * P],
                                          adj_buf[j // 8][:, k * P:(k + 1) * P], ident[:])
                    tp.then_inc(turned_psum[j % 2], 1)
                    if j:
                        add_group(j - 1)
                add_group(15)
                pe.wait_ge(x1_ready, t + 1 + CREDIT)
                pe.wait_ge(kept_ready, t + CREDIT)
                pe.transpose(bank[4][:, 0:P], kept[:, 0:C], ident[:]).then_inc(x1T_psum, 1)
                pe.wait_ge(x1T_ready, t + 1)
                pe.matmul(bank[5][:, 0:P], W_all[:, 0:C], x1T[:], start=True, stop=True)
                pe.matmul(bank[5][:, P:2 * P], W_all[:, C:2 * C], x1T[:], start=True, stop=True)
                pe.matmul(bank[5][:, 2 * P:], x1T[:], W_all[:, 2 * C:], start=True, stop=True)\
                  .then_inc(proj_ready, 1)

            pe.wait_ge(kept_ready, T + CREDIT)
            with pe.Fori(0, T) as t:
                pe.wait_ge(q_ready, t + 1)
                for h in range(H):
                    u = t * H + h
                    for j in range(16):
                        pe.wait_ge(s_masked[j % 2], u * 8 + j // 2 + CREDIT)
                        pe.matmul(bank[6 + j % 2][:], qz[:, h, :], kT[:, j * BANK:(j + 1) * BANK],
                                  start=True, stop=True).then_inc(s_psum[j % 2], 1)

                    def add_values(j):
                        pe.wait_ge(p_sbuf[j % 2], u * 8 + (j // 2 + 1) + CREDIT)
                        for i in range(4):
                            m = 4 * j + i
                            mm = pe.matmul(bank[2][:, 0:HC], turned[j % 2][:, i * P:(i + 1) * P],
                                           v_rows[:, m, h * HC:(h + 1) * HC], start=m == 0, stop=m == T - 1)
                        mm.then_inc(p_used[j % 2], 1)
                        return mm

                    pe.wait_ge(exp_ready, u + 1)
                    for j in range(16):
                        pe.wait_ge(p_sbuf[j % 2], u * 8 + j // 2 + CREDIT)
                        for i in range(4):
                            k = 4 * j + i
                            tp = pe.transpose(bank[j % 2][:, i * P:(i + 1) * P], scores[:, k * P:(k + 1) * P],
                                              ident[:])
                        tp.then_inc(p_psum[j % 2], 1)
                        if j == 1:
                            pe.wait_ge(head_used, u + CREDIT)
                        if j:
                            add_values(j - 1)
                    add_values(15)

        @block.vector
        def _(dve):
            step = Steps(dve, dve_step)
            dve.wait_ge(loaded, 16 * N_CONST)
            dve.tensor_scalar(neg_time[:], time_col[:], -1.0, None, ALU.mult).then_inc(neg_ready, 1)
            dve.wait_ge(decay_ready, 2)
            for h in range(2):
                dve.wait_ge(adj_summed, (h + 1) * T)
                for k in range(8):
                    for i in range(4):
                        t = h * (T // 2) + 4 * k + i
                        last = dve.scalar_tensor_tensor(
                            out=yT[:, t * P:(t + 1) * P], in0=bank[k][:, i * P:(i + 1) * P],
                            scalar=decay0[:, t:t + 1], in1=decay1[:], op0=ALU.mult, op1=ALU.mult)
                    last.then_inc(y_scaled, 1)
            for j in range(0, 16, 2):
                dve.wait_ge(y_turned[0], j // 2 + 1)
                dve.tensor_copy(y_rows[:, 4 * j:4 * j + 4, :].rearrange("p t c -> p (t c)"), bank[0][:])\
                   .then_inc(y_copied[0], 1)

            def normalise(src, dst, asked, given, count):
                step(dve.reduce_sum(moments[:, 0:1], src, AX_X))
                step(dve.tensor_scalar(moments[:, 0:1], moments[:, 0:1], 1.0 / C, None, ALU.mult))
                step(dve.tensor_scalar(centred[:], src, moments[:, 0:1], None, ALU.subtract))
                step(dve.scalar_tensor_tensor(out=squares[:], in0=centred[:], scalar=1.0, in1=centred[:],
                                              op0=ALU.mult, op1=ALU.mult, accum_out=moments[:, 1:2]))
                dve.tensor_scalar(moments[:, 1:2], moments[:, 1:2], 1.0 / C, EPS, ALU.mult, ALU.add).then_inc(asked, 1)
                dve.wait_ge(given, count)
                return dve.tensor_scalar(dst, centred[:], rstd[:], None, ALU.mult)

            with dve.Fori(0, T) as t:
                step.enter(t, 5)
                for j in range(8):
                    dve.wait_ge(turned_psum[0], t * 8 + (j + 1) + CREDIT)
                    dve.wait_ge(turned_used[0], t * 8 + j + CREDIT)
                    dve.tensor_copy(turned[0][:], bank[0][:]).then_inc(turned_sbuf[0], 1)
                dve.wait_ge(turned_used[1], t * 8 + 8 + CREDIT)
                dve.wait_ge(x_landed, t * 16 + 16)
                step(dve.tensor_tensor(pre[:], bank[2][:, 0:C], x_tile[:], ALU.add))
                dve.wait_ge(kept_stored, t * 16 + CREDIT)
                normalise(pre[:], kept[:, 0:C], var_ready, rstd_ready, t + 1).then_inc(x1_ready, 1)
                dve.wait_ge(proj_ready, t + 1)
                dve.tensor_scalar(qT[:, bass.ds(t * P, P)], bank[5][:, 0:P], bq_col[:], None, ALU.add)
                dve.tensor_scalar(kT[:, bass.ds(t * P, P)], bank[5][:, P:2 * P], bk_col[:], None, ALU.add)
                dve.tensor_tensor(v_rows[:, t, :], bank[5][:, 2 * P:3 * P], b_vs[:, 0:C], ALU.add)
                dve.tensor_tensor(kept[:, C:], bank[5][:, 3 * P:], b_vs[:, C:], ALU.add).then_inc(kept_ready, 1)
                step.leave(T)

            for h in range(H):
                last = dve.memset(qz[:, h, :], 0.0)
            step(last)
            with dve.Fori(0, T) as t:
                step.enter(t, 1 + 3 * H + 10)
                for half in range(2):
                    dve.wait_ge(block_landed[half], t * 16 + 16 * (T + 1))
                    last = dve.tensor_scalar(adj_buf[half], adj_buf[half], 0.0, -FAR, ALU.is_equal, ALU.mult)
                step(last)
                for h in range(H):
                    rows = slice(h * HC, (h + 1) * HC)
                    last = dve.tensor_copy(qz[rows, h, :], qT[rows, bass.ds(t * P, P)])
                last.then_inc(q_ready, 1)
                for h in range(H):
                    u = t * H + h
                    dve.wait_ge(p_psum[0], u * 8 + CREDIT)
                    dve.wait_ge(p_psum[1], u * 8 + CREDIT)
                    for j in range(16):
                        dve.wait_ge(s_psum[j % 2], u * 8 + (j // 2 + 1))
                        dve.scalar_tensor_tensor(
                            out=scores[:, j * BANK:(j + 1) * BANK], in0=bank[6 + j % 2][:], scalar=SCALE,
                            in1=adj_buf[j // 8][:, (j % 8) * BANK:(j % 8 + 1) * BANK],
                            op0=ALU.mult, op1=ALU.add).then_inc(s_masked[j % 2], 1)
                    dve.wait_ge(s_masked[0], u * 8 + 8 + CREDIT)
                    dve.wait_ge(s_masked[1], u * 8 + 8 + CREDIT)
                    step(dve.reduce_max(rowmax[:, h:h + 1], scores, AX_X))
                    step(dve.tensor_scalar(shift[:, h:h + 1], rowmax[:, h:h + 1], -FAR / 2, -1.0, ALU.is_gt, ALU.mult))
                    dve.tensor_tensor(shift[:, h:h + 1], shift[:, h:h + 1], rowmax[:, h:h + 1], ALU.mult)\
                       .then_inc(shift_ready, 1)
                    for j in range(8):
                        dve.wait_ge(p_psum[0], u * 8 + (j + 1) + CREDIT)
                        dve.wait_ge(p_used[0], u * 8 + j + CREDIT)
                        dve.tensor_copy(turned[0][:], bank[0][:]).then_inc(p_sbuf[0], 1)
                    dve.wait_ge(exp_ready, u + 1)
                    step(dve.scalar_tensor_tensor(out=inv[:, h:h + 1], in0=den[:, h:h + 1], scalar=0.0,
                                                  in1=den[:, h:h + 1], op0=ALU.is_equal, op1=ALU.add))
                    dve.reciprocal(inv[:, h:h + 1], inv[:, h:h + 1]).then_inc(inv_ready, 1)
                    dve.wait_ge(inv_ready, u + 1)
                    dve.wait_ge(p_used[1], u * 8 + 8 + CREDIT)
                    dve.tensor_scalar(cat[:, 0:C].rearrange("p (c h) -> p h c", h=H)[:, h, :], bank[2][:, 0:HC],
                                      inv[:, h:h + 1], None, ALU.mult).then_inc(head_used, 1)
                dve.wait_ge(head_used, t * H + H + CREDIT)
                dve.wait_ge(kept_back, t * 16 + 16)
                dve.tensor_copy(cat[:, C:2 * C], kept_in[:, C:])
                step(dve.tensor_tensor(cat[:, 2 * C:], cat[:, 0:C], kept_in[:, C:], ALU.subtract))
                step(dve.tensor_tensor(prod[:], cat[:], Wb_rows[:], ALU.mult))
                dve.reduce_sum(beta[:, 0:1], prod[:], AX_X).then_inc(logit_ready, 1)
                dve.wait_ge(beta_ready, t + 1)
                step(dve.tensor_scalar(beta[:, 2:3], beta[:, 1:2], 1.0, None, ALU.add))
                step(dve.reciprocal(beta[:, 3:4], beta[:, 2:3]))
                step(dve.scalar_tensor_tensor(out=prod[:, 0:C], in0=cat[:, 2 * C:], scalar=beta[:, 3:4],
                                              in1=cat[:, 0:C], op0=ALU.mult, op1=ALU.subtract))
                step(dve.tensor_tensor(pre[:], kept_in[:, 0:C], prod[:, 0:C], ALU.subtract))
                dve.wait_ge(res_stored, t * 16 + CREDIT)
                normalise(pre[:], res[:], var2_ready, rstd2_ready, t + 1).then_inc(res_ready, 1)
                step.leave(T)


_INS = ["x", "adj", "L0_gnn_mass", "L0_gnn_evals0", "L0_gnn_evals1", "L0_gnn_diffusion_time",
        "L1_gnn_Wq", "L1_gnn_bq", "L1_gnn_Wk", "L1_gnn_bk", "L1_gnn_Wv", "L1_gnn_bv",
        "L1_gnn_Ws", "L1_gnn_bs", "L1_gnn_Wb"]


def kernel(**inputs):
    import numpy as _np
    import concourse.bacc as _bacc
    from concourse import mybir as _mybir
    from concourse.bass_utils import run_bass_kernel_spmd as _run

    nc = _bacc.Bacc("TRN2", target_bir_lowering=False, num_devices=1)
    arrays, args = {}, []
    laid_out = {"L0_gnn_mass": (T, P), "L0_gnn_diffusion_time": (2, C), "L1_gnn_bq": (1, C), "L1_gnn_bk": (1, C)}
    for name in _INS:
        a = _np.asarray(inputs[name])
        if name in laid_out:
            a = a.reshape(laid_out[name]).T
        a = _np.ascontiguousarray(a)
        arrays[f"in_{name}_dram"] = a
        args.append(nc.dram_tensor(f"in_{name}_dram", a.shape, _mybir.dt.from_np(a.dtype), kind="ExternalInput").ap())
    args.append(nc.dram_tensor("out_dram", (N, C), F32, kind="ExternalOutput").ap())
    build_program(nc, *args)
    r = _run(nc, [arrays], core_ids=[0])
    return r.results[0]["out_dram"]
```

```python
from contextlib import ExitStack

import numpy as np

import concourse.bass as bass
from concourse import mybir

F32 = mybir.dt.float32
BF16 = mybir.dt.bfloat16
U32 = mybir.dt.uint32
I32 = mybir.dt.int32
ALU = mybir.AluOpType
ACT = mybir.ActivationFunctionType
AX_X = mybir.AxisListType.X

P = 128
N = 8192
C = 128
T = N // P
V0, V1 = 64, 128
H, HC = 4, 32
BANK = 512
HALF = N // 2
NBUF = 4
EPS = 1e-5
SCALE = float(1.0 / np.sqrt(np.float32(HC)))
FAR = 1e30
CREDIT = 1

SEG = 1024
SEGS = HALF // SEG
NCAND = N // SEG * 8
SLOTS = [k for k, tiles in ((29, 1), (16, 1), (15, 1), (14, 2), (13, 4), (12, 4), (11, 7), (10, 8), (9, 9), (8, 9),
                            (7, 8), (6, 5), (5, 3), (4, 2)) for _ in range(tiles)]
assert len(SLOTS) == T and SLOTS == sorted(SLOTS, reverse=True)
FEWEST, NCLS = 4, 16
MOST = FEWEST + NCLS - 1
ROW = 260
AT_COL, AT_VAL, AT_ID = C, C + NCAND, C + 2 * NCAND
SLOT0 = [sum(SLOTS[:j]) for j in range(T + 1)]
PARITY_SLOTS = [sum(SLOTS[j % 2:j + 1:2]) for j in range(T)]


def runs():
    key = [(SLOTS[j], SLOTS[min(j + 2, T - 1)], j >= T - 2, j < 4) for j in range(T)]
    out = []
    for j in range(T):
        if j and key[j] == key[j - 1]:
            out[-1][1] += 1
        else:
            out.append([j, 1])
    return out


def for_tiles(eng, body, step=None, per=None):
    for first, tiles in runs():
        pairs = tiles // 2 if tiles >= 4 else 0
        if pairs:
            with eng.Fori(0, pairs) as turn:
                if step:
                    step.enter(turn, per(first) + per(first + 1))
                body(first, turn)
                body(first + 1, turn)
                if step:
                    step.leave(pairs)
        for j in range(first + 2 * pairs, first + tiles):
            body(j, 0)


class Steps:

    def __init__(self, eng, sem, carrier=None):
        self.eng, self.sem, self.base, self.turn, self.k, self.carrier = eng, sem, 0, None, 0, carrier

    def __call__(self, ins, carry=False):
        self.k += 1
        ins.then_inc(self.sem, 1)
        past = self.base if self.turn is None else self.turn * self.per + self.base
        self.eng.wait_ge(self.sem, past + self.k)
        if carry and self.turn is not None:
            self.eng.sem_inc(self.carrier, 1)

    def enter(self, turn, per):
        self.base += self.k
        self.turn, self.per, self.k = turn, per, 0

    def leave(self, turns):
        assert self.k == self.per, (self.k, self.per)
        self.base += turns * self.per
        self.turn, self.k = None, 0


def build_program(nc, x, adj, mass, evals0, evals1, diff_time, Wq, bq, bq_row, Wk, bk, bk_row, Wv, bv, Ws, bs, Wb, out):
    with ExitStack() as ctx:
        def sb(name, shape, dt=F32):
            return ctx.enter_context(nc.sbuf_tensor(name, shape, dt))

        def sem(name):
            return ctx.enter_context(nc.semaphore(name))

        keep = nc.dram_tensor("kept_rows", [N, 2 * C], F32, kind="Internal").ap()
        records = nc.dram_tensor("records", [N, ROW], F32, kind="Internal").ap()
        y_table = nc.dram_tensor("y_table", [N, C], F32, kind="Internal").ap()
        kv_table = nc.dram_tensor("kv_table", [N, 2 * C], F32, kind="Internal").ap()
        xsq_rows = nc.dram_tensor("xsq_rows", [N, 3 * C], F32, kind="Internal").ap()

        REC = T * ROW
        arena = sb("arena", [P, 3 * N + REC])
        yT, kT = arena[:, 0:N], arena[:, 0:N]
        rec_all = arena[:, N:N + REC]
        rec = rec_all.rearrange("p (t w) -> p t w", w=ROW)
        qT = arena[:, N:2 * N]
        v_rows = arena[:, 2 * N:3 * N].rearrange("p (t c) -> p t c", c=C)
        adj0 = N + REC
        adj_buf = [arena[:, adj0 + b * HALF:adj0 + (b + 1) * HALF] for b in range(NBUF)]
        y_rows = arena[:, adj0 + N:].rearrange("p (t c) -> p t c", c=C)
        scores = arena[:, adj0 + N:]
        free_at = [0]

        def carve(words):
            free_at[0] += words
            return arena[:, free_at[0] - words:free_at[0]]

        KMAX = SLOTS[0]
        drawn_y = [carve(KMAX * C) for _ in range(2)]
        free_at[0] = adj0
        y_prod = carve(KMAX * C)
        match = carve(KMAX * NCAND)
        free_at[0] = 0
        drawn_kv = [carve(KMAX * 2 * C) for _ in range(2)]
        qk_prod = carve(KMAX * C)
        ev_prod = carve(KMAX * C)
        pre_all = carve(N).rearrange("p (t c) -> p t c", c=C)
        assert free_at[0] <= adj0 + N
        S_ALL = SLOT0[T]
        cols_all = carve(S_ALL).bitcast(U32)
        valid_all = carve(S_ALL)
        lower_all = carve(S_ALL)
        assert free_at[0] <= adj0 + N
        free_at[0] = adj0 + N
        xsq = [carve(3 * C) for b in range(2)]
        kv_out = [carve(2 * C) for b in range(2)]
        xsq_in = [carve(3 * C) for b in range(2)]
        catf = [carve(3 * C) for b in range(2)]
        out_rows = [carve(C) for b in range(2)]
        att = carve(C)
        logits = carve(KMAX * H)
        assert free_at[0] <= 3 * N + REC

        ident = sb("ident", [P, P])
        mass_sb = sb("mass_sb", [P, T])
        time_col = sb("time_col", [P, 2])
        neg_time = sb("neg_time", [P, 2])
        ev0 = sb("ev0", [P, V0])
        ev1 = sb("ev1", [P, V1])
        decay0 = sb("decay0", [P, V0])
        decay1 = sb("decay1", [P, V1])
        W_all = sb("W_all", [P, 4 * C])
        b_all = sb("b_all", [P, 4 * C])
        bq_col = sb("bq_col", [P, 1])
        bk_col = sb("bk_col", [P, 1])
        Wb_rows = sb("Wb_rows", [P, 3 * C])
        xm = [sb(f"xm{b}", [P, C]) for b in range(NBUF)]
        minus_half = sb("minus_half", [P, 1])
        x_tile = sb("x_tile", [P, C])
        pre = sb("pre", [P, C])
        kept = sb("kept", [P, 2 * C])
        x1T = sb("x1T", [P, C])
        centred = sb("centred", [P, C])
        squares = sb("squares", [P, C])
        moments = sb("moments", [P, 2])
        rstd = sb("rstd", [P, 1])
        qz = sb("qz", [P, H, P])
        rowmax = sb("rowmax", [P, H])
        shift = sb("shift", [P, H])
        den = sb("den", [P, H])
        inv = sb("inv", [P, H])
        cat = sb("cat", [P, 3 * C])
        prod = sb("prod", [P, 3 * C])
        beta = sb("beta", [P, 4])
        res = sb("res", [P, C])
        kept_in = sb("kept_in", [P, 2 * C])

        junk_words = [sb(f"junk{b}", [P, HALF // 2]) for b in range(2)]
        junk = [words[:].bitcast(BF16) for words in junk_words]
        turned = [junk_words[0][:, b * BANK:(b + 1) * BANK] for b in range(2)]
        cand_val = [sb(f"cand_val{b}", [P, SEGS * 8]) for b in range(NBUF)]
        cand_col = [sb(f"cand_col{b}", [P, SEGS * 8], U32) for b in range(NBUF)]
        seg_start = [sb(f"seg_start{h}", [P, SEGS * 8]) for h in range(2)]
        cand_float = sb("cand_float", [P, SEGS * 8])
        n_pos = sb("n_pos", [P, 2, T])
        n_neg = sb("n_neg", [P, 2, T])
        tri = sb("tri", [P, P], BF16)
        ones = sb("ones", [P, P], BF16)
        cls = sb("cls", [P, NCLS])
        limit = sb("limit", [P, NCLS])
        degree = sb("degree", [P, T])
        clipped = sb("clipped", [P, T])
        rank = sb("rank", [P, T])
        rank_u = sb("rank_u", [P, T], U32)
        bad = sb("bad", [P, 8])
        bad_cls = sb("bad_cls", [P, NCLS])
        bad_sum = sb("bad_sum", [P, 1])
        bad_bf = sb("bad_bf", [P, 1], BF16)
        flag = sb("flag", [1, 1], I32)
        iota_i = sb("iota_i", [P, T], I32)
        id_all = sb("id_all", [P, T], U32)
        codes = [sb(f"codes{b}", [P, NCAND]) for b in range(3)]
        top = sb("top", [P, 32])
        draw_cols = [sb(f"draw_cols{b}", [P, KMAX], U32) for b in range(2)]
        weight = [sb(f"weight{b}", [P, KMAX]) for b in range(2)]
        stats = sb("stats", [P, 6])
        mom = sb("mom", [P, 2])
        root = sb("root", [P, 1])
        mean_all = sb("mean_all", [P, T])
        var_all = sb("var_all", [P, T])
        eps_col = sb("eps_col", [P, 1])
        draw_id = [sb(f"draw_id{b}", [P, 1], U32) for b in range(2)]
        small = sb("small", [P, 24])
        rstd_all = sb("rstd_all", [P, T])
        NHOT = NCLS * T
        hot = junk[1][:, 0:NHOT]
        up = arena[:, adj0:adj0 + NHOT]
        place = arena[:, adj0 + NHOT:adj0 + 2 * NHOT]
        no_rows = sb("no_rows", [P, BANK], BF16)

        bank = [ctx.enter_context(nc.psum_tensor(f"bank{b}", [P, BANK], F32)) for b in range(8)]

        loaded = sem("loaded")
        ident_ready = sem("ident_ready")
        adj_landed = [sem(f"adj_landed{b}") for b in range(NBUF)]
        xm_ready = sem("xm_ready")
        adj_summed = sem("adj_summed")
        decay_ready = sem("decay_ready")
        neg_ready = sem("neg_ready")
        y_scaled = sem("y_scaled")
        y_turned = [sem(f"y_turned{b}") for b in range(2)]
        y_copied = [sem(f"y_copied{b}") for b in range(2)]
        dve_step = sem("dve_step")
        block_landed = [sem(f"block_landed{b}") for b in range(2)]
        x_landed = sem("x_landed")
        turned_psum = [sem(f"turned_psum{b}") for b in range(2)]
        turned_sbuf = [sem(f"turned_sbuf{b}") for b in range(2)]
        turned_used = [sem(f"turned_used{b}") for b in range(2)]
        var_ready = sem("var_ready")
        rstd_ready = sem("rstd_ready")
        x1_ready = sem("x1_ready")
        x1T_psum = sem("x1T_psum")
        x1T_ready = sem("x1T_ready")
        proj_ready = sem("proj_ready")
        kept_ready = sem("kept_ready")
        kept_stored = sem("kept_stored")
        kept_back = sem("kept_back")
        q_ready = sem("q_ready")
        s_psum = [sem(f"s_psum{b}") for b in range(2)]
        s_masked = [sem(f"s_masked{b}") for b in range(2)]
        shift_ready = sem("shift_ready")
        exp_ready = sem("exp_ready")
        p_psum = [sem(f"p_psum{b}") for b in range(2)]
        p_sbuf = [sem(f"p_sbuf{b}") for b in range(2)]
        p_used = [sem(f"p_used{b}") for b in range(2)]
        head_ready = sem("head_ready")
        head_used = sem("head_used")
        inv_ready = sem("inv_ready")
        logit_ready = sem("logit_ready")
        beta_ready = sem("beta_ready")
        var2_ready = sem("var2_ready")
        rstd2_ready = sem("rstd2_ready")
        res_ready = sem("res_ready")
        res_stored = sem("res_stored")
        N_CONST = 16
        N_READY = 2 * SEGS + 4 + 2 * NCLS
        carried = sem("carried")
        carried_pool = sem("carried_pool")
        carried_sp = sem("carried_sp")
        cand_max = sem("cand_max")
        cand_ready = sem("cand_ready")
        cand_used = sem("cand_used")
        counted = sem("counted")
        const_ready = sem("const_ready")
        pool_step = sem("pool_step")
        hot_ready = sem("hot_ready")
        before_ready = sem("before_ready")
        candidates_counted = sem("candidates_counted")
        rank_ready = sem("rank_ready")
        bad_ready = sem("bad_ready")
        bad_psum = sem("bad_psum")
        flag_ready = sem("flag_ready")
        y_stored = sem("y_stored")
        sorted_out = sem("sorted_out")
        record_back = sem("record_back")
        fast_step = sem("fast_step")
        draw_ready = sem("draw_ready")
        drawn = [sem(f"drawn{b}") for b in range(2)]
        drawn_used = sem("drawn_used")
        mean_ready = sem("mean_ready")
        root_ready = sem("root_ready")
        row_ready = sem("row_ready")
        rowT_psum = sem("rowT_psum")
        rowT_ready = sem("rowT_ready")
        lin_ready = sem("lin_ready")
        lin_used = sem("lin_used")
        xsq_stored = [sem(f"xsq_stored{b}") for b in range(2)]
        kv_stored = [sem(f"kv_stored{b}") for b in range(2)]
        xsq_back = [sem(f"xsq_back{b}") for b in range(2)]
        draw2_ready = sem("draw2_ready")
        drawn2 = [sem(f"drawn2{b}") for b in range(2)]
        drawn2_used = sem("drawn2_used")
        xr_copied = sem("xr_copied")
        arg_ready = sem("arg_ready")
        e_ready = sem("e_ready")
        z_ready = sem("z_ready")
        ez_ready = sem("ez_ready")
        blended = sem("blended")
        power_ready = sem("power_ready")
        final_ready = sem("final_ready")
        final_stored = [sem(f"final_stored{b}") for b in range(2)]



        def dense_sync(sp):
            sp.wait_ge(adj_summed, 2 * T)
            with sp.Fori(0, T) as t:
                for half in range(2):
                    sp.wait_ge(turned_psum[1], (t * 8 + 4 * half - 4 if half else t * 8) + CREDIT)
                    sp.dma_start(adj_buf[half], adj[bass.ds(t * P, P), half * HALF:(half + 1) * HALF])\
                      .then_inc(block_landed[half], 16)
                sp.wait_ge(x1_ready, t + CREDIT)
                sp.dma_start(x_tile[:], x[bass.ds(t * P, P), :]).then_inc(x_landed, 16)
                sp.wait_ge(kept_ready, t + 1 + CREDIT)
                sp.dma_start(keep[bass.ds(t * P, P), :], kept[:]).then_inc(kept_stored, 16)
            sp.wait_ge(kept_stored, 16 * T + CREDIT)
            with sp.Fori(0, T) as t:
                sp.wait_ge(s_masked[0], t * (H * 8) + CREDIT)
                sp.wait_ge(s_masked[1], t * (H * 8) + CREDIT)
                for half in range(2):
                    sp.dma_start(adj_buf[half], adj[bass.ds(t * P, P), half * HALF:(half + 1) * HALF])\
                      .then_inc(block_landed[half], 16)
                sp.wait_ge(res_ready, t + CREDIT)
                sp.dma_start(kept_in[:], keep[bass.ds(t * P, P), :]).then_inc(kept_back, 16)
                sp.wait_ge(res_ready, t + 1 + CREDIT)
                sp.dma_start(out[bass.ds(t * P, P), :], res[:]).then_inc(res_stored, 16)
            sp.wait_ge(res_stored, 16 * T + CREDIT)

        def dense_pool(pool):
            with pool.Fori(0, T) as t:
                pool.wait_ge(var_ready, t + 1)
                pool.tensor_tensor(rstd[:], moments[:, 1:2], minus_half[:], ALU.pow).then_inc(rstd_ready, 1)
            with pool.Fori(0, T) as t:
                pool.wait_ge(var2_ready, t + 1)
                pool.tensor_tensor(rstd[:], moments[:, 1:2], minus_half[:], ALU.pow).then_inc(rstd2_ready, 1)

        def dense_scalar(act):
            with act.Fori(0, T) as t:
                for j in range(8):
                    act.wait_ge(turned_psum[1], t * 8 + (j + 1) + CREDIT)
                    act.wait_ge(turned_used[1], t * 8 + j + CREDIT)
                    act.activation(turned[1], bank[1][:], ACT.Copy).then_inc(turned_sbuf[1], 1)
                act.wait_ge(x1T_psum, t + 1)
                act.activation(x1T[:], bank[4][:, 0:P], ACT.Copy).then_inc(x1T_ready, 1)
            with act.Fori(0, T) as t:
                for h in range(H):
                    act.wait_ge(shift_ready, t * H + (h + 1))
                    act.activation(scores, scores, ACT.Exp, bias=shift[:, h:h + 1],
                                   accum_out=den[:, h:h + 1]).then_inc(exp_ready, 1)
                    for j in range(8):
                        act.wait_ge(p_psum[1], (t * H + h) * 8 + (j + 1) + CREDIT)
                        act.wait_ge(p_used[1], (t * H + h) * 8 + j + CREDIT)
                        act.activation(turned[1], bank[1][:], ACT.Copy).then_inc(p_sbuf[1], 1)
                act.wait_ge(logit_ready, t + 1)
                act.activation(beta[:, 1:2], beta[:, 0:1], ACT.Exp, scale=-1.0).then_inc(beta_ready, 1)

        def dense_tensor(pe):
            with pe.Fori(0, T) as t:
                def add_group(j):
                    pe.wait_ge(turned_sbuf[j % 2], t * 8 + (j // 2 + 1) + CREDIT)
                    for i in range(4):
                        m = 4 * j + i
                        mm = pe.matmul(bank[2][:, 0:C], turned[j % 2][:, i * P:(i + 1) * P], y_rows[:, m, :],
                                       start=m == 0, stop=m == T - 1)
                    mm.then_inc(turned_used[j % 2], 1)
                    return mm

                for j in range(16):
                    if j % 8 == 0:
                        pe.wait_ge(block_landed[j // 8], t * 16 + 16)
                    pe.wait_ge(turned_sbuf[j % 2], t * 8 + j // 2 + CREDIT)
                    for i in range(4):
                        k = 4 * (j % 8) + i
                        tp = pe.transpose(bank[j % 2][:, i * P:(i + 1) * P],
                                          adj_buf[j // 8][:, k * P:(k + 1) * P], ident[:])
                    tp.then_inc(turned_psum[j % 2], 1)
                    if j:
                        add_group(j - 1)
                add_group(15)
                pe.wait_ge(x1_ready, t + 1 + CREDIT)
                pe.wait_ge(kept_ready, t + CREDIT)
                pe.transpose(bank[4][:, 0:P], kept[:, 0:C], ident[:]).then_inc(x1T_psum, 1)
                pe.wait_ge(x1T_ready, t + 1)
                pe.matmul(bank[5][:, 0:P], W_all[:, C:2 * C], x1T[:], start=True, stop=True)
                pe.matmul(bank[5][:, P:2 * P], W_all[:, 2 * C:3 * C], x1T[:], start=True, stop=True)
                pe.matmul(bank[5][:, 2 * P:3 * P], x1T[:], W_all[:, 3 * C:], start=True, stop=True)
                pe.matmul(bank[5][:, 3 * P:], x1T[:], W_all[:, 0:C], start=True, stop=True)\
                  .then_inc(proj_ready, 1)

            pe.wait_ge(kept_ready, T + CREDIT)
            with pe.Fori(0, T) as t:
                pe.wait_ge(q_ready, t + 1)
                for h in range(H):
                    u = t * H + h
                    for j in range(16):
                        pe.wait_ge(s_masked[j % 2], u * 8 + j // 2 + CREDIT)
                        pe.matmul(bank[6 + j % 2][:], qz[:, h, :], kT[:, j * BANK:(j + 1) * BANK],
                                  start=True, stop=True).then_inc(s_psum[j % 2], 1)

                    def add_values(j):
                        pe.wait_ge(p_sbuf[j % 2], u * 8 + (j // 2 + 1) + CREDIT)
                        for i in range(4):
                            m = 4 * j + i
                            mm = pe.matmul(bank[2][:, 0:HC], turned[j % 2][:, i * P:(i + 1) * P],
                                           v_rows[:, m, h * HC:(h + 1) * HC], start=m == 0, stop=m == T - 1)
                        mm.then_inc(p_used[j % 2], 1)
                        return mm

                    pe.wait_ge(exp_ready, u + 1)
                    for j in range(16):
                        pe.wait_ge(p_sbuf[j % 2], u * 8 + j // 2 + CREDIT)
                        for i in range(4):
                            k = 4 * j + i
                            tp = pe.transpose(bank[j % 2][:, i * P:(i + 1) * P], scores[:, k * P:(k + 1) * P],
                                              ident[:])
                        tp.then_inc(p_psum[j % 2], 1)
                        if j == 1:
                            pe.wait_ge(head_used, u + CREDIT)
                        if j:
                            add_values(j - 1)
                    add_values(15)

        def dense_vector(dve, step):
            def normalise(src, dst, asked, given, count):
                step(dve.reduce_sum(moments[:, 0:1], src, AX_X))
                step(dve.tensor_scalar(moments[:, 0:1], moments[:, 0:1], 1.0 / C, None, ALU.mult))
                step(dve.tensor_scalar(centred[:], src, moments[:, 0:1], None, ALU.subtract))
                step(dve.scalar_tensor_tensor(out=squares[:], in0=centred[:], scalar=1.0, in1=centred[:],
                                              op0=ALU.mult, op1=ALU.mult, accum_out=moments[:, 1:2]))
                dve.tensor_scalar(moments[:, 1:2], moments[:, 1:2], 1.0 / C, EPS, ALU.mult, ALU.add).then_inc(asked, 1)
                dve.wait_ge(given, count)
                return dve.tensor_scalar(dst, centred[:], rstd[:], None, ALU.mult)

            with dve.Fori(0, T) as t:
                step.enter(t, 5)
                for j in range(8):
                    dve.wait_ge(turned_psum[0], t * 8 + (j + 1) + CREDIT)
                    dve.wait_ge(turned_used[0], t * 8 + j + CREDIT)
                    dve.tensor_copy(turned[0], bank[0][:]).then_inc(turned_sbuf[0], 1)
                dve.wait_ge(turned_used[1], t * 8 + 8 + CREDIT)
                dve.wait_ge(x_landed, t * 16 + 16)
                step(dve.tensor_tensor(pre[:], bank[2][:, 0:C], x_tile[:], ALU.add))
                dve.wait_ge(kept_stored, t * 16 + CREDIT)
                normalise(pre[:], kept[:, 0:C], var_ready, rstd_ready, t + 1).then_inc(x1_ready, 1)
                dve.wait_ge(proj_ready, t + 1)
                dve.tensor_scalar(qT[:, bass.ds(t * P, P)], bank[5][:, 0:P], bq_col[:], None, ALU.add)
                dve.tensor_scalar(kT[:, bass.ds(t * P, P)], bank[5][:, P:2 * P], bk_col[:], None, ALU.add)
                dve.tensor_tensor(v_rows[:, t, :], bank[5][:, 2 * P:3 * P], b_all[:, 3 * C:], ALU.add)
                dve.tensor_tensor(kept[:, C:], bank[5][:, 3 * P:], b_all[:, 0:C], ALU.add).then_inc(kept_ready, 1)
                step.leave(T)

            for h in range(H):
                last = dve.memset(qz[:, h, :], 0.0)
            step(last)
            with dve.Fori(0, T) as t:
                step.enter(t, 1 + 3 * H + 10)
                for half in range(2):
                    dve.wait_ge(block_landed[half], t * 16 + 16 * (T + 1))
                    last = dve.tensor_scalar(adj_buf[half], adj_buf[half], 0.0, -FAR, ALU.is_equal, ALU.mult)
                step(last)
                for h in range(H):
                    rows = slice(h * HC, (h + 1) * HC)
                    last = dve.tensor_copy(qz[rows, h, :], qT[rows, bass.ds(t * P, P)])
                last.then_inc(q_ready, 1)
                for h in range(H):
                    u = t * H + h
                    dve.wait_ge(p_psum[0], u * 8 + CREDIT)
                    dve.wait_ge(p_psum[1], u * 8 + CREDIT)
                    for j in range(16):
                        dve.wait_ge(s_psum[j % 2], u * 8 + (j // 2 + 1))
                        dve.scalar_tensor_tensor(
                            out=scores[:, j * BANK:(j + 1) * BANK], in0=bank[6 + j % 2][:], scalar=SCALE,
                            in1=adj_buf[j // 8][:, (j % 8) * BANK:(j % 8 + 1) * BANK],
                            op0=ALU.mult, op1=ALU.add).then_inc(s_masked[j % 2], 1)
                    dve.wait_ge(s_masked[0], u * 8 + 8 + CREDIT)
                    dve.wait_ge(s_masked[1], u * 8 + 8 + CREDIT)
                    step(dve.reduce_max(rowmax[:, h:h + 1], scores, AX_X))
                    step(dve.tensor_scalar(shift[:, h:h + 1], rowmax[:, h:h + 1], -FAR / 2, -1.0, ALU.is_gt, ALU.mult))
                    dve.tensor_tensor(shift[:, h:h + 1], shift[:, h:h + 1], rowmax[:, h:h + 1], ALU.mult)\
                       .then_inc(shift_ready, 1)
                    for j in range(8):
                        dve.wait_ge(p_psum[0], u * 8 + (j + 1) + CREDIT)
                        dve.wait_ge(p_used[0], u * 8 + j + CREDIT)
                        dve.tensor_copy(turned[0], bank[0][:]).then_inc(p_sbuf[0], 1)
                    dve.wait_ge(exp_ready, u + 1)
                    step(dve.scalar_tensor_tensor(out=inv[:, h:h + 1], in0=den[:, h:h + 1], scalar=0.0,
                                                  in1=den[:, h:h + 1], op0=ALU.is_equal, op1=ALU.add))
                    dve.reciprocal(inv[:, h:h + 1], inv[:, h:h + 1]).then_inc(inv_ready, 1)
                    dve.wait_ge(inv_ready, u + 1)
                    dve.wait_ge(p_used[1], u * 8 + 8 + CREDIT)
                    dve.tensor_scalar(cat[:, 0:C].rearrange("p (c h) -> p h c", h=H)[:, h, :], bank[2][:, 0:HC],
                                      inv[:, h:h + 1], None, ALU.mult).then_inc(head_used, 1)
                dve.wait_ge(head_used, t * H + H + CREDIT)
                dve.wait_ge(kept_back, t * 16 + 16)
                dve.tensor_copy(cat[:, C:2 * C], kept_in[:, C:])
                step(dve.tensor_tensor(cat[:, 2 * C:], cat[:, 0:C], kept_in[:, C:], ALU.subtract))
                step(dve.tensor_tensor(prod[:], cat[:], Wb_rows[:], ALU.mult))
                dve.reduce_sum(beta[:, 0:1], prod[:], AX_X).then_inc(logit_ready, 1)
                dve.wait_ge(beta_ready, t + 1)
                step(dve.tensor_scalar(beta[:, 2:3], beta[:, 1:2], 1.0, None, ALU.add))
                step(dve.reciprocal(beta[:, 3:4], beta[:, 2:3]))
                step(dve.scalar_tensor_tensor(out=prod[:, 0:C], in0=cat[:, 2 * C:], scalar=beta[:, 3:4],
                                              in1=cat[:, 0:C], op0=ALU.mult, op1=ALU.subtract))
                step(dve.tensor_tensor(pre[:], kept_in[:, 0:C], prod[:, 0:C], ALU.subtract))
                dve.wait_ge(res_stored, t * 16 + CREDIT)
                normalise(pre[:], res[:], var2_ready, rstd2_ready, t + 1).then_inc(res_ready, 1)
                step.leave(T)




        def at(first, turn):
            return first + 2 * turn

        def stored(first, turn):
            return 16 * (first // 2) + 16 * turn

        def slots_of(first, turn):
            return bass.ds(SLOT0[first] + 2 * SLOTS[first] * turn, SLOTS[first])

        def carry(eng, carrier, turn):
            if not isinstance(turn, int):
                eng.sem_inc(carrier, 1)

        def sparse_sync(sp):
            sp.wait_ge(sorted_out, 16 * T)
            with sp.Fori(0, T) as t:
                sp.dma_start(rec[:, t, :], records[bass.ds(t * P, P), :]).then_inc(record_back, 16)
                sp.wait_ge(record_back, t * 16 + 16)
                carry(sp, carried_sp, t)

            for p in range(2):
                sp.wait_ge(xsq_stored[p], 16 * (T // 2))

            def load(first, turn):
                if first >= 2:
                    sp.wait_ge(blended, at(first, turn) - 1)
                carry(sp, carried_sp, turn)
                sp.dma_start(xsq_in[first % 2], xsq_rows[bass.ds(at(first, turn) * P, P), :])\
                  .then_inc(xsq_back[first % 2], 16)

            for_tiles(sp, load)
            for p in range(2):
                sp.wait_ge(final_stored[p], 16 * (T // 2))

        def gather(pool, table, cols, s, to, done):
            pool.indirect_dma_start(out=to, out_offset=None, in_=table,
                                    in_offset=bass.IndirectOffsetOnAxis(ap=cols[:, s:s + 1], axis=0)).then_inc(done, 16)

        def scatter(pool, table, ids, of, done):
            pool.indirect_dma_start(out=table, out_offset=bass.IndirectOffsetOnAxis(ap=ids, axis=0), in_=of,
                                    in_offset=None).then_inc(done, 16)

        def sparse_pool(pool):
            pool.wait_ge(rank_ready, 1)
            for t in range(T):
                scatter(pool, records, rank_u[:, t:t + 1], rec[:, t, :], sorted_out)
            pool.wait_ge(y_stored, 16 * 4)

            def store_kv(first, turn):
                p = first % 2
                pool.wait_ge(lin_used, at(first, turn) + 1)
                carry(pool, carried_pool, turn)
                scatter(pool, kv_table, draw_id[p][:], kv_out[p], kv_stored[p])

            def draw(first, turn):
                p = first % 2
                pool.wait_ge(draw_ready, at(first, turn) + 1)
                if first >= 2:
                    pool.wait_ge(drawn_used, at(first, turn) - 1)
                carry(pool, carried_pool, turn)
                for s in range(SLOTS[first]):
                    gather(pool, y_table, draw_cols[p], s, drawn_y[p][:, s * C:(s + 1) * C], drawn[p])
                if first >= 2:
                    store_kv(first - 2, turn)

            for_tiles(pool, draw)
            store_kv(T - 2, 0)
            store_kv(T - 1, 0)
            for p in range(2):
                pool.wait_ge(kv_stored[p], 16 * (T // 2))

            def power(first, turn):
                t = at(first, turn)
                pool.wait_ge(blended, t + 1)
                pool.tensor_tensor(rstd_all[:, bass.ds(t, 1)], var_all[:, bass.ds(t, 1)], minus_half[:], ALU.pow)\
                    .then_inc(power_ready, 1)

            def store_out(first, turn):
                p = first % 2
                pool.wait_ge(final_ready, at(first, turn) + 1)
                carry(pool, carried_pool, turn)
                scatter(pool, out, draw_id[p][:], out_rows[p], final_stored[p])

            def draw2(first, turn):
                p = first % 2
                pool.wait_ge(draw2_ready, at(first, turn) + 1)
                if first >= 2:
                    pool.wait_ge(drawn2_used, at(first, turn) - 1)
                carry(pool, carried_pool, turn)
                for s in range(SLOTS[first]):
                    gather(pool, kv_table, draw_cols[p], s, drawn_kv[p][:, s * 2 * C:(s + 1) * 2 * C], drawn2[p])
                if first >= 2:
                    power(first - 2, turn)
                if first >= 3:
                    store_out(first - 3, turn)

            for_tiles(pool, draw2)
            power(T - 2, 0)
            store_out(T - 3, 0)
            power(T - 1, 0)
            store_out(T - 2, 0)
            store_out(T - 1, 0)

        def sparse_scalar(act):
            def store_xsq(first, turn):
                p, t = first % 2, at(first, turn)
                act.wait_ge(lin_used, t + 1)
                act.dma_start(xsq_rows[bass.ds(t * P, P), :], xsq[p]).then_inc(xsq_stored[p], 16)

            def layer0(first, turn):
                t = at(first, turn)
                act.wait_ge(mean_ready, t + 1)
                act.activation(root[:], mom[:, 1:2], ACT.Sqrt, bias=eps_col[:]).then_inc(root_ready, 1)
                if first >= 1:
                    store_xsq(first - 1, turn)
                act.wait_ge(rowT_psum, t + 1)
                act.activation(x1T[:], bank[4][:, 0:P], ACT.Copy).then_inc(rowT_ready, 1)

            for_tiles(act, layer0)
            store_xsq(T - 1, 0)

            def layer1(first, turn):
                p, t = first % 2, at(first, turn)
                act.wait_ge(xsq_back[p], stored(first, turn) + 16)
                if first >= 2:
                    act.wait_ge(blended, t - 1)
                act.activation(catf[p][:, C:2 * C], xsq_in[p][:, C:2 * C], ACT.Copy).then_inc(xr_copied, 1)
                act.wait_ge(arg_ready, t + 1)
                e = logits[:, 0:SLOTS[first] * H]
                act.activation(e, e, ACT.Exp).then_inc(e_ready, 1)
                act.wait_ge(z_ready, t + 1)
                act.activation(small[:, 20:21], small[:, 16:17], ACT.Exp, scale=-1.0).then_inc(ez_ready, 1)

            for_tiles(act, layer1)

        def sparse_tensor(pe):
            def layer0(first, turn):
                p, t = first % 2, at(first, turn)
                pe.wait_ge(row_ready, t + 1)
                pe.transpose(bank[4][:, 0:P], xsq[p][:, 0:C], ident[:]).then_inc(rowT_psum, 1)
                pe.wait_ge(rowT_ready, t + 1)
                pe.matmul(bank[6 + p][:], x1T[:], W_all[:], start=True, stop=True).then_inc(lin_ready, 1)

            for_tiles(pe, layer0)

        def sparse_vector(dve):
            step = Steps(dve, fast_step, carried)

            def wide(ap, n):
                return ap.unsqueeze(2).to_broadcast([P, ap.shape[1], n])

            def over(ap, n):
                return ap.unsqueeze(1).to_broadcast([P, n, ap.shape[1]])

            def fill(first, turn):
                p, t, K = first % 2, at(first, turn), SLOTS[first]
                rounds = -(-K // 8)
                dve.wait_ge(record_back, t * 16 + 16)
                step(dve.scalar_tensor_tensor(out=codes[0][:], in0=rec[:, t, AT_VAL:AT_VAL + NCAND], scalar=0.0,
                                              in1=rec[:, t, AT_COL:AT_COL + NCAND], op0=ALU.is_gt, op1=ALU.mult), True)
                held = codes[0]
                for r in range(rounds):
                    eight = top[:, 8 * r:8 * r + 8]
                    step(dve.max(eight, held[:]), r + 1 < rounds)
                    if r + 1 < rounds:
                        rest = codes[1 + r % 2]
                        step(dve.match_replace(rest[:], eight, held[:], 0.0), True)
                        held = rest
                same = match[:, 0:K * NCAND].rearrange("p (s c) -> p s c", c=NCAND)
                step(dve.tensor_tensor(same, wide(top[:, 0:K], NCAND), over(codes[0][:], K), ALU.is_equal))
                step(dve.tensor_tensor(same, same, over(rec[:, t, AT_VAL:AT_VAL + NCAND], K), ALU.mult))
                dve.tensor_reduce(weight[p][:, 0:K], same, AX_X, ALU.add)
                at_slots = slots_of(first, turn)
                dve.tensor_scalar(valid_all[:, at_slots], top[:, 0:K], 0.0, None, ALU.is_gt)
                dve.tensor_scalar(lower_all[:, at_slots], top[:, 0:K], 0.0, -FAR, ALU.is_equal, ALU.mult)
                dve.tensor_copy(id_all[:, bass.ds(t, 1)], rec[:, t, AT_ID:AT_ID + 1])
                step(dve.tensor_scalar(draw_cols[p][:, 0:K], top[:, 0:K], 1.0, 0.0, ALU.subtract, ALU.max))
                dve.tensor_copy(cols_all[:, at_slots], draw_cols[p][:, 0:K]).then_inc(draw_ready, 1)

            def diffuse(first, turn):
                p, t, K = first % 2, at(first, turn), SLOTS[first]
                dve.wait_ge(drawn[p], K * 16 * turn + 16 * PARITY_SLOTS[first])
                prod_y = y_prod[:, 0:K * C].rearrange("p (s c) -> p s c", c=C)
                dve.tensor_tensor(prod_y, drawn_y[p][:, 0:K * C].rearrange("p (s c) -> p s c", c=C),
                                  wide(weight[p][:, 0:K], C), ALU.mult).then_inc(drawn_used, 1)
                dve.wait_ge(drawn_used, t + 1)
                step(dve.tensor_reduce(pre[:], prod_y.rearrange("p s c -> p c s"), AX_X, ALU.add))
                step(dve.tensor_tensor(pre[:], pre[:], rec[:, t, 0:C], ALU.add))
                step(dve.bn_stats(stats[:], pre[:]), True)
                dve.bn_aggr(mom[:], stats[:]).then_inc(mean_ready, 1)

            def take_lin(first, turn):
                p, t = first % 2, at(first, turn)
                dve.wait_ge(lin_ready, t + 1)
                if first >= 2:
                    dve.wait_ge(kv_stored[p], stored(first, turn))
                dve.tensor_tensor(xsq[p][:, C:], bank[6 + p][:, 0:2 * C], b_all[:, 0:2 * C], ALU.add)
                dve.tensor_copy(draw_id[p][:], id_all[:, bass.ds(t, 1)])
                dve.tensor_tensor(kv_out[p], bank[6 + p][:, 2 * C:], b_all[:, 2 * C:], ALU.add).then_inc(lin_used, 1)

            def normalise_x1(first, turn):
                p, t = first % 2, at(first, turn)
                dve.wait_ge(root_ready, t + 1)
                if first >= 2:
                    dve.wait_ge(xsq_stored[p], stored(first, turn))
                step(dve.reciprocal(rstd[:], root[:]))
                dve.tensor_scalar(xsq[p][:, 0:C], pre[:], mom[:, 0:1], rstd[:], ALU.subtract, ALU.mult)\
                   .then_inc(row_ready, 1)

            def layer0(first, turn):
                diffuse(first, turn)
                if first >= 1:
                    take_lin(first - 1, turn)
                normalise_x1(first, turn)
                if first + 2 < T:
                    fill(first + 2, turn)

            fill(0, 0)
            fill(1, 0)
            for_tiles(dve, layer0, step, lambda first: 4 + 2 * -(-SLOTS[first + 2] // 8) + 3)
            take_lin(T - 1, 0)

            def refill(first, turn):
                p, K = first % 2, SLOTS[first]
                dve.tensor_copy(draw_cols[p][:, 0:K], cols_all[:, slots_of(first, turn)]).then_inc(draw2_ready, 1)

            def attend(first, turn):
                p, t, K = first % 2, at(first, turn), SLOTS[first]
                at_slots = slots_of(first, turn)
                dve.wait_ge(drawn2[p], K * 16 * turn + 16 * PARITY_SLOTS[first])
                dve.wait_ge(xsq_back[p], stored(first, turn) + 16)
                kv = drawn_kv[p][:, 0:K * 2 * C].rearrange("p (s c) -> p s c", c=2 * C)
                qk = qk_prod[:, 0:K * C]
                step(dve.tensor_tensor(qk.rearrange("p (s c) -> p s c", c=C), kv[:, :, 0:C],
                                       over(xsq_in[p][:, 2 * C:], K), ALU.mult))
                lg = logits[:, 0:K * H]
                lg3 = lg.rearrange("p (s h) -> p s h", h=H)
                lgT = lg.rearrange("p (s h) -> p h s", h=H)
                step(dve.tensor_reduce(lg, qk.rearrange("p (x c) -> p x c", c=HC), AX_X, ALU.add))
                step(dve.scalar_tensor_tensor(out=lg3, in0=lg3, scalar=SCALE, in1=wide(lower_all[:, at_slots], H),
                                              op0=ALU.mult, op1=ALU.add))
                step(dve.tensor_reduce(small[:, 0:H], lgT, AX_X, ALU.max))
                dve.tensor_tensor(lg3, lg3, over(small[:, 0:H], K), ALU.subtract).then_inc(arg_ready, 1)
                dve.wait_ge(e_ready, t + 1)
                step(dve.tensor_tensor(lg3, lg3, wide(valid_all[:, at_slots], H), ALU.mult))
                ev = ev_prod[:, 0:K * C]
                dve.tensor_tensor(
                    ev.rearrange("p (s h c) -> p s h c", h=H, c=HC),
                    kv[:, :, C:].rearrange("p s (h c) -> p s h c", c=HC),
                    lg3.unsqueeze(3).to_broadcast([P, K, H, HC]), ALU.mult).then_inc(drawn2_used, 1)
                step(dve.tensor_reduce(small[:, 4:8], lgT, AX_X, ALU.add))
                step(dve.scalar_tensor_tensor(out=small[:, 8:12], in0=small[:, 4:8], scalar=0.0, in1=small[:, 4:8],
                                              op0=ALU.is_equal, op1=ALU.add))
                dve.reciprocal(small[:, 12:16], small[:, 8:12])
                step(dve.tensor_reduce(att, ev.rearrange("p (s c) -> p c s", c=C), AX_X, ALU.add))
                step(dve.tensor_tensor(catf[p][:, 0:C].rearrange("p (c h) -> p h c", h=H),
                                       att.rearrange("p (h c) -> p h c", h=H), wide(small[:, 12:16], HC), ALU.mult))
                dve.wait_ge(xr_copied, t + 1)
                step(dve.tensor_tensor(catf[p][:, 2 * C:], catf[p][:, 0:C], catf[p][:, C:2 * C], ALU.subtract))
                dve.scalar_tensor_tensor(out=cat[:], in0=catf[p], scalar=1.0, in1=Wb_rows[:], op0=ALU.mult,
                                         op1=ALU.mult, accum_out=small[:, 16:17]).then_inc(z_ready, 1)
                dve.wait_ge(ez_ready, t + 1)
                step(dve.tensor_scalar(small[:, 21:22], small[:, 20:21], 1.0, None, ALU.add))
                step(dve.reciprocal(small[:, 22:23], small[:, 21:22]))
                step(dve.scalar_tensor_tensor(out=att, in0=catf[p][:, 2 * C:], scalar=small[:, 22:23],
                                              in1=catf[p][:, 0:C], op0=ALU.mult, op1=ALU.subtract))
                step(dve.tensor_tensor(pre_all[:, t, :], xsq_in[p][:, 0:C], att, ALU.subtract), True)
                step(dve.bn_stats(stats[:], pre_all[:, t, :]), True)
                step(dve.bn_aggr(mom[:], stats[:]))
                dve.tensor_copy(mean_all[:, bass.ds(t, 1)], mom[:, 0:1])
                dve.tensor_scalar(var_all[:, bass.ds(t, 1)], mom[:, 1:2], EPS, None, ALU.add).then_inc(blended, 1)

            def finish(first, turn):
                p, t = first % 2, at(first, turn)
                dve.wait_ge(power_ready, t + 1)
                if first >= 2:
                    dve.wait_ge(final_stored[p], stored(first, turn))
                dve.tensor_copy(draw_id[p][:], id_all[:, bass.ds(t, 1)])
                dve.tensor_scalar(out_rows[p], pre_all[:, t, :], mean_all[:, bass.ds(t, 1)],
                                  rstd_all[:, bass.ds(t, 1)], ALU.subtract, ALU.mult).then_inc(final_ready, 1)

            def layer1(first, turn):
                attend(first, turn)
                if first >= 2:
                    finish(first - 2, turn)
                if first + 2 < T:
                    refill(first + 2, turn)

            refill(0, 0)
            refill(1, 0)
            for_tiles(dve, layer1, step, lambda first: 16)
            finish(T - 2, 0)
            finish(T - 1, 0)



        block = ctx.enter_context(nc.Block())

        @block.sync
        def _(sp):
            for to, of in (
                (rec[:, :, 0:C], x.rearrange("(t p) c -> p t c", p=P)),
                (mass_sb[:], mass),
                (time_col[:], diff_time),
                (ev0[:], evals0.partition_broadcast(P)),
                (ev1[:], evals1.partition_broadcast(P)),
                (W_all[:, 0:C], Ws), (W_all[:, C:2 * C], Wq), (W_all[:, 2 * C:3 * C], Wk), (W_all[:, 3 * C:], Wv),
                (b_all[:, 0:C], bs.partition_broadcast(P)), (b_all[:, C:2 * C], bq_row.partition_broadcast(P)),
                (b_all[:, 2 * C:3 * C], bk_row.partition_broadcast(P)), (b_all[:, 3 * C:], bv.partition_broadcast(P)),
                (bq_col[:], bq), (bk_col[:], bk),
                (Wb_rows[:], Wb.rearrange("c a -> (a c)").partition_broadcast(P)),
            ):
                sp.dma_start(to, of).then_inc(loaded, 16)

            def load_block(h, g, b):
                rows = bass.ds((g * NBUF + b) * P, P)
                sp.dma_start(adj_buf[b], adj[rows, h * HALF:(h + 1) * HALF]).then_inc(adj_landed[b], 16)

            for b in range(NBUF):
                load_block(0, 0, b)
            for h in range(2):
                with sp.Fori(1 - h, T // NBUF) as g:
                    for b in range(NBUF):
                        past = h * T + g * NBUF + (b + 1 - NBUF)
                        sp.wait_ge(adj_summed, past)
                        sp.wait_ge(cand_ready, past)
                        sp.wait_ge(counted, past)
                        load_block(h, g, b)

            sp.wait_ge(y_copied[0], 8)
            sp.wait_ge(y_copied[1], 8)
            for part in range(4):
                tiles = slice(part * T // 4, (part + 1) * T // 4)
                sp.dma_start(y_table[part * N // 4:(part + 1) * N // 4, :].rearrange("(t p) c -> p t c", p=P),
                             y_rows[:, tiles, :]).then_inc(y_stored, 16)
            sp.wait_ge(flag_ready, 1)
            dense = sp.value_load(flag[0:1, 0:1], min_val=0, max_val=1)
            with sp.If(dense):
                dense_sync(sp)
            with sp.Else():
                sparse_sync(sp)

        @block.gpsimd
        def _(pool):
            for credited in (*turned_psum, *turned_sbuf, *turned_used, x1_ready, kept_ready, kept_stored, *s_masked,
                             res_ready, *p_psum, *p_sbuf, *p_used, head_used, res_stored):
                pool.sem_inc(credited, CREDIT)
            pool.memset(ident[:], 0.0).then_inc(ident_ready, 1)
            pool.memset(minus_half[:], -0.5).then_inc(ident_ready, 1)
            pool.wait_ge(ident_ready, 2)
            pool.affine_select(out=ident[:], in_=ident[:], compare_op=ALU.not_equal, fill=1.0, base=0,
                               pattern=[[-1, P]], channel_multiplier=1).then_inc(ident_ready, 1)
            step = Steps(pool, pool_step, carried_pool)
            for h in range(2):
                for k in range(SEGS):
                    pool.memset(seg_start[h][:, 8 * k:8 * k + 8], float(h * HALF + k * SEG + 1)).then_inc(const_ready, 1)
            pool.memset(ones[:], 1.0).then_inc(const_ready, 1)
            pool.memset(no_rows[:], 0.0).then_inc(const_ready, 1)
            pool.memset(eps_col[:], EPS).then_inc(const_ready, 1)
            step(pool.memset(tri[:], 1.0))
            pool.affine_select(out=tri[:], in_=tri[:], compare_op=ALU.is_gt, fill=0.0, base=0,
                               pattern=[[1, P]], channel_multiplier=-1).then_inc(const_ready, 1)
            for k in range(NCLS):
                pool.memset(cls[:, k:k + 1], float(MOST - k)).then_inc(const_ready, 1)
                fit = sum(n >= (MOST - k if k else SLOTS[0]) for n in SLOTS) if k < NCLS - 1 else T
                pool.memset(limit[:, k:k + 1], float(fit * P)).then_inc(const_ready, 1)
            step(pool.iota(iota_i[:], [[P, T]], base=0, channel_multiplier=1))
            pool.wait_ge(loaded, 16 * N_CONST)
            step(pool.tensor_copy(rec[:, :, AT_ID:AT_ID + 1].rearrange("p t a -> p (t a)"), iota_i[:]))
            step(pool.memset(rec[:, :, AT_ID + 1:ROW], 0.0))
            pool.wait_ge(const_ready, N_READY)

            def file(h, g, b):
                t = g * NBUF + b
                pool.wait_ge(cand_ready, g * NBUF + (h * T + b + 1))
                pool.sem_inc(carried_pool, 1)
                at = h * SEGS * 8
                step(pool.tensor_copy(cand_float[:], cand_col[b][:]))
                step(pool.tensor_tensor(rec[:, t, AT_COL + at:AT_COL + at + SEGS * 8], cand_float[:], seg_start[h][:],
                                        ALU.add))
                pool.tensor_copy(rec[:, t, AT_VAL + at:AT_VAL + at + SEGS * 8], cand_val[b][:]).then_inc(cand_used, 1)

            for h in range(2):
                with pool.Fori(0, T // NBUF) as g:
                    step.enter(g, 2 * NBUF)
                    for b in range(NBUF):
                        file(h, g, b)
                    step.leave(T // NBUF)
            pool.wait_ge(flag_ready, 1)
            dense = pool.value_load(flag[0:1, 0:1], min_val=0, max_val=1)
            with pool.If(dense):
                dense_pool(pool)
            with pool.Else():
                sparse_pool(pool)

        @block.scalar
        def _(act):
            act.wait_ge(neg_ready, 1)
            act.activation(decay0[:], ev0[:], ACT.Exp, scale=neg_time[:, 0:1]).then_inc(decay_ready, 1)
            act.activation(decay1[:], ev1[:], ACT.Exp, scale=neg_time[:, 1:2]).then_inc(decay_ready, 1)

            def weigh(g, b):
                t = g * NBUF + b
                act.activation(xm[b][:], rec[:, t, 0:C], ACT.Copy, scale=mass_sb[:, bass.ds(t, 1)])\
                   .then_inc(xm_ready, 1)

            def count(h, g, b):
                t = g * NBUF + b
                act.wait_ge(adj_landed[b], g * 16 + 16 * (h * (T // NBUF) + 1))
                done = g * NBUF + (h * T + b)
                if h or b or not isinstance(g, int):
                    act.wait_ge(counted, done)
                act.activation(junk[0], adj_buf[b], ACT.Sign, accum_out=n_pos[:, h, bass.ds(t, 1)])
                act.activation(junk[1], adj_buf[b], ACT.Relu, scale=-1.0, accum_out=n_neg[:, h, bass.ds(t, 1)])\
                   .then_inc(counted, 1)

            act.wait_ge(loaded, 16 * N_CONST)
            for b in range(NBUF):
                weigh(0, b)
            for b in range(NBUF):
                count(0, 0, b)
            for h in range(2):
                with act.Fori(1 - h, T // NBUF) as g:
                    for b in range(NBUF):
                        act.wait_ge(adj_summed, h * T + g * NBUF + (b + 1 - NBUF))
                        weigh(g, b)
                        count(h, g, b)
            act.wait_ge(cand_used, 2 * T)
            act.wait_ge(counted, 2 * T)
            act.activation(junk[0].rearrange("p (t c) -> p t c", c=NCAND), rec[:, :, AT_VAL:AT_VAL + NCAND],
                           ACT.Sign, accum_out=bad[:, 0:1]).then_inc(candidates_counted, 1)
            for j in range(1, 16, 2):
                act.wait_ge(y_turned[1], j // 2 + 1)
                act.activation(y_rows[:, 4 * j:4 * j + 4, :].rearrange("p t c -> p (t c)"), bank[1][:], ACT.Copy)\
                   .then_inc(y_copied[1], 1)
            act.wait_ge(flag_ready, 1)
            dense = act.value_load(flag[0:1, 0:1], min_val=0, max_val=1)
            with act.If(dense):
                dense_scalar(act)
            with act.Else():
                sparse_scalar(act)

        @block.tensor
        def _(pe):
            def add_block(h, g, b, first, last):
                pe.wait_ge(adj_landed[b], g * 16 + 16 * (h * (T // NBUF) + 1))
                pe.wait_ge(xm_ready, g * NBUF + (h * T + b + 1))
                for k in range(8):
                    if h and first:
                        pe.wait_ge(y_scaled, k + 1)
                    mm = pe.matmul(bank[k][:], xm[b][:], adj_buf[b][:, k * BANK:(k + 1) * BANK],
                                   start=first, stop=last)
                mm.then_inc(adj_summed, 1)

            for h in range(2):
                for b in range(NBUF):
                    add_block(h, 0, b, b == 0, False)
                with pe.Fori(1, T // NBUF - 1) as g:
                    for b in range(NBUF):
                        add_block(h, g, b, False, False)
                for b in range(NBUF):
                    add_block(h, T // NBUF - 1, b, False, b == NBUF - 1)
            pe.wait_ge(y_scaled, 16)
            pe.wait_ge(ident_ready, 3)
            for j in range(16):
                if j >= 2:
                    pe.wait_ge(y_copied[j % 2], j // 2)
                for i in range(4):
                    tp = pe.transpose(bank[j % 2][:, i * P:(i + 1) * P], yT[:, (4 * j + i) * P:(4 * j + i + 1) * P],
                                      ident[:])
                tp.then_inc(y_turned[j % 2], 1)
            for p in range(2):
                pe.wait_ge(y_copied[p], 8)

            pe.wait_ge(const_ready, N_READY)
            pe.wait_ge(hot_ready, 1)
            for k in range(NCLS * T // BANK):
                pe.matmul(bank[2 + k][:], tri[:], hot[:, k * BANK:(k + 1) * BANK], start=True, stop=True)
            for k in range(NCLS * T // BANK):
                mm = pe.matmul(bank[4 + k][:], ones[:], hot[:, k * BANK:(k + 1) * BANK], start=True, stop=True)
            mm.then_inc(before_ready, 1)
            pe.wait_ge(bad_ready, 1)
            pe.matmul(bank[6][0:1, 0:1], bad_bf[:], ones[:, 0:1], start=True, stop=True).then_inc(bad_psum, 1)
            pe.wait_ge(flag_ready, 1)
            dense = pe.value_load(flag[0:1, 0:1], min_val=0, max_val=1)
            with pe.If(dense):
                dense_tensor(pe)
            with pe.Else():
                sparse_tensor(pe)

        @block.vector
        def _(dve):
            step = Steps(dve, dve_step)
            dve.wait_ge(loaded, 16 * N_CONST)
            dve.tensor_scalar(neg_time[:], time_col[:], -1.0, None, ALU.mult).then_inc(neg_ready, 1)
            dve.wait_ge(decay_ready, 2)
            def find(h, g, b):
                done = g * NBUF + (h * T + b)
                dve.wait_ge(adj_landed[b], g * 16 + 16 * (h * (T // NBUF) + 1))
                if h or not isinstance(g, int):
                    dve.wait_ge(cand_used, done - (NBUF - 1))
                if not isinstance(g, int):
                    dve.sem_inc(carried, 1)
                for k in range(SEGS):
                    last = dve.max(cand_val[b][:, 8 * k:8 * k + 8], adj_buf[b][:, k * SEG:(k + 1) * SEG])
                last.then_inc(cand_max, 1)
                dve.wait_ge(cand_max, done + 1)
                if not isinstance(g, int):
                    dve.sem_inc(carried, 1)
                for k in range(SEGS):
                    last = dve.max_index(cand_col[b][:, 8 * k:8 * k + 8], cand_val[b][:, 8 * k:8 * k + 8],
                                         adj_buf[b][:, k * SEG:(k + 1) * SEG])
                last.then_inc(cand_ready, 1)

            for h in range(2):
                if h == 0:
                    for b in range(NBUF):
                        find(0, 0, b)
                with dve.Fori(1 - h, T // NBUF) as g:
                    for b in range(NBUF):
                        find(h, g, b)
                dve.wait_ge(adj_summed, (h + 1) * T)
                for k in range(8):
                    for i in range(4):
                        t = h * (T // 2) + 4 * k + i
                        last = dve.scalar_tensor_tensor(
                            out=yT[:, t * P:(t + 1) * P], in0=bank[k][:, i * P:(i + 1) * P],
                            scalar=decay0[:, t:t + 1], in1=decay1[:], op0=ALU.mult, op1=ALU.mult)
                    last.then_inc(y_scaled, 1)

            dve.wait_ge(cand_ready, 2 * T)
            dve.wait_ge(counted, 2 * T)
            dve.wait_ge(const_ready, N_READY)
            step(dve.tensor_tensor(degree[:], n_pos[:, 0, :], n_pos[:, 1, :], ALU.add))
            step(dve.tensor_scalar(clipped[:], degree[:], float(FEWEST), float(MOST), ALU.max, ALU.min))
            dve.tensor_tensor(hot.rearrange("p (k t) -> p k t", k=NCLS), clipped[:].unsqueeze(1).to_broadcast([P, NCLS, T]),
                              cls[:].unsqueeze(2).to_broadcast([P, NCLS, T]), ALU.is_equal).then_inc(hot_ready, 1)
            for j in range(0, 16, 2):
                dve.wait_ge(y_turned[0], j // 2 + 1)
                dve.tensor_copy(y_rows[:, 4 * j:4 * j + 4, :].rearrange("p t c -> p (t c)"), bank[0][:])\
                   .then_inc(y_copied[0], 1)
            dve.wait_ge(before_ready, 1)
            dve.wait_ge(hot_ready, 1)
            NB = NCLS * T // BANK
            for k in range(NB):
                step(dve.tensor_tensor_scan(up[:, k * BANK:(k + 1) * BANK], bank[4 + k][:], no_rows[:],
                                            0.0 if k == 0 else up[:, k * BANK - 1:k * BANK], ALU.add, ALU.add))
            for k in range(NB):
                cut = slice(k * BANK, (k + 1) * BANK)
                last = dve.tensor_tensor(place[:, cut], up[:, cut], bank[4 + k][:], ALU.subtract)
            step(last)
            for k in range(NB):
                cut = slice(k * BANK, (k + 1) * BANK)
                last = dve.tensor_tensor(place[:, cut], place[:, cut], bank[2 + k][:], ALU.add)
            step(last)
            step(dve.tensor_tensor(place, place, hot, ALU.mult))
            step(dve.tensor_reduce(rank[:], place.rearrange("p (k t) -> p t k", k=NCLS), AX_X, ALU.add))
            dve.tensor_copy(rank_u[:], rank[:]).then_inc(rank_ready, 1)
            step(dve.tensor_tensor(bad_cls[:], up.rearrange("p (k t) -> p k t", k=NCLS)[:, :, T - 1], limit[:], ALU.is_gt))
            step(dve.reduce_sum(bad[:, 1:2], bad_cls[:], AX_X))
            step(dve.reduce_sum(bad[:, 2:3], degree[:], AX_X))
            dve.wait_ge(candidates_counted, 1)
            step(dve.tensor_tensor(bad[:, 3:4], bad[:, 2:3], bad[:, 0:1], ALU.not_equal))
            step(dve.tensor_reduce(bad[:, 4:5], n_neg[:], mybir.AxisListType.XY, ALU.max))
            step(dve.tensor_scalar(bad[:, 4:5], bad[:, 4:5], 0.0, None, ALU.not_equal))
            step(dve.reduce_max(bad[:, 5:6], degree[:], AX_X))
            step(dve.tensor_scalar(bad[:, 5:6], bad[:, 5:6], float(SLOTS[0]), None, ALU.is_gt))
            step(dve.tensor_tensor(bad[:, 3:4], bad[:, 3:4], bad[:, 1:2], ALU.add))
            step(dve.reduce_sum(bad_sum[:], bad[:, 3:6], AX_X))
            dve.tensor_copy(bad_bf[:], bad_sum[:]).then_inc(bad_ready, 1)
            dve.wait_ge(bad_psum, 1)
            dve.tensor_scalar(flag[:], bank[6][0:1, 0:1], 0.0, None, ALU.is_gt).then_inc(flag_ready, 1)
            dve.wait_ge(flag_ready, 1)
            dense = dve.value_load(flag[0:1, 0:1], min_val=0, max_val=1)
            with dve.If(dense):
                dense_vector(dve, step)
            with dve.Else():
                sparse_vector(dve)


_INS = ["x", "adj", "L0_gnn_mass", "L0_gnn_evals0", "L0_gnn_evals1", "L0_gnn_diffusion_time",
        "L1_gnn_Wq", "L1_gnn_bq", "L1_gnn_bq_row", "L1_gnn_Wk", "L1_gnn_bk", "L1_gnn_bk_row", "L1_gnn_Wv", "L1_gnn_bv",
        "L1_gnn_Ws", "L1_gnn_bs", "L1_gnn_Wb"]


def kernel(**inputs):
    import numpy as _np
    import concourse.bacc as _bacc
    from concourse import mybir as _mybir
    from concourse.bass_utils import run_bass_kernel_spmd as _run

    nc = _bacc.Bacc("TRN2", target_bir_lowering=False, num_devices=1)
    arrays, args = {}, []
    laid_out = {"L0_gnn_mass": (T, P), "L0_gnn_diffusion_time": (2, C), "L1_gnn_bq": (1, C), "L1_gnn_bk": (1, C)}
    for name in _INS:
        a = _np.asarray(inputs[name.removesuffix("_row")])
        if name in laid_out:
            a = a.reshape(laid_out[name]).T
        a = _np.ascontiguousarray(a)
        arrays[f"in_{name}_dram"] = a
        args.append(nc.dram_tensor(f"in_{name}_dram", a.shape, _mybir.dt.from_np(a.dtype), kind="ExternalInput").ap())
    args.append(nc.dram_tensor("out_dram", (N, C), F32, kind="ExternalOutput").ap())
    build_program(nc, *args)
    r = _run(nc, [arrays], core_ids=[0])
    return r.results[0]["out_dram"]
```

```python
from contextlib import ExitStack

import numpy as np

import concourse.bass as bass
from concourse import mybir

F32 = mybir.dt.float32
BF16 = mybir.dt.bfloat16
U32 = mybir.dt.uint32
I32 = mybir.dt.int32
ALU = mybir.AluOpType
ACT = mybir.ActivationFunctionType
AX_X = mybir.AxisListType.X

P = 128
N = 8192
C = 128
T = N // P
V0, V1 = 64, 128
H, HC = 4, 32
BANK = 512
HALF = N // 2
NBUF = 4
EPS = 1e-5
SCALE = float(1.0 / np.sqrt(np.float32(HC)))
FAR = 1e30
CREDIT = 1

SEG = 1024
SEGS = HALF // SEG
NCAND = N // SEG * 8
SLOTS = [k - 1 for k, tiles in ((25, 1), (16, 1), (15, 1), (14, 2), (13, 4), (12, 4), (11, 7), (10, 8), (9, 9), (8, 9),
                            (7, 8), (6, 5), (5, 3), (4, 2)) for _ in range(tiles)]
assert len(SLOTS) == T and SLOTS == sorted(SLOTS, reverse=True)
FEWEST, NCLS = 4, 16
MOST = FEWEST + NCLS - 1
ROW = 260
YW = C + 1
AT_COL, AT_VAL, AT_ID = C, C + NCAND, C + 2 * NCAND
WIDE0 = [sum(SLOTS[:j]) + j for j in range(T + 1)]
RING = 3
WAYS_SLOTS = {ways: [sum(SLOTS[j % ways:j + 1:ways]) for j in range(T)] for ways in (2, RING)}


def runs(key):
    out = []
    for j in range(T):
        if j and key(j) == key(j - 1):
            out[-1][1] += 1
        else:
            out.append([j, 1])
    return out


def for_tiles(eng, body, ways, step=None, per=None, after=None):
    if ways == 2:
        parts = runs(lambda j: (SLOTS[j], SLOTS[min(j + 2, T - 1)], j >= T - 2, j < 4))
    else:
        parts = runs(lambda j: (SLOTS[j], j < 4))
    for first, tiles in parts:
        turns = tiles // ways if tiles >= 2 * ways else 0
        if turns:
            assert first >= 2 * ways
            with eng.Fori(0, turns) as turn:
                if step:
                    step.enter(turn, sum(per(first + k) for k in range(ways)))
                for k in range(ways):
                    body(first + k, turn)
                if step:
                    step.leave(turns)
        for j in range(first + ways * turns, first + tiles):
            body(j, 0)
        if after:
            after(first + tiles)


class Steps:

    def __init__(self, eng, sem, carrier=None):
        self.eng, self.sem, self.base, self.turn, self.k, self.carrier = eng, sem, 0, None, 0, carrier

    def __call__(self, ins, carry=False):
        self.k += 1
        ins.then_inc(self.sem, 1)
        past = self.base if self.turn is None else self.turn * self.per + self.base
        self.eng.wait_ge(self.sem, past + self.k)
        if carry and self.turn is not None:
            self.eng.sem_inc(self.carrier, 1)

    def mark(self, ins):
        self.k += 1
        ins.then_inc(self.sem, 1)
        return self.k

    def need(self, place):
        past = self.base if self.turn is None else self.turn * self.per + self.base
        self.eng.wait_ge(self.sem, past + place)

    def enter(self, turn, per):
        self.base += self.k
        self.turn, self.per, self.k = turn, per, 0

    def leave(self, turns):
        assert self.k == self.per, (self.k, self.per)
        self.base += turns * self.per
        self.turn, self.k = None, 0


def build_program(nc, x, adj, mass, evals0, evals1, diff_time, Wq, bq, bq_row, Wk, bk, bk_row, Wv, bv, Ws, bs, Wb, out):
    with ExitStack() as ctx:
        def sb(name, shape, dt=F32):
            return ctx.enter_context(nc.sbuf_tensor(name, shape, dt))

        def sem(name):
            return ctx.enter_context(nc.semaphore(name))

        keep = nc.dram_tensor("kept_rows", [N, 2 * C], F32, kind="Internal").ap()
        records = nc.dram_tensor("records", [N, ROW], F32, kind="Internal").ap()
        y_table = nc.dram_tensor("y_table", [N, YW], F32, kind="Internal").ap()
        kv_table = nc.dram_tensor("kv_table", [N, 2 * C], F32, kind="Internal").ap()
        xsq_rows = nc.dram_tensor("xsq_rows", [N, 3 * C], F32, kind="Internal").ap()

        REC = T * ROW
        arena = sb("arena", [P, 3 * N + REC + T])
        yT, kT = arena[:, 0:N], arena[:, 0:N]
        rec_all = arena[:, N:N + REC]
        rec = rec_all.rearrange("p (t w) -> p t w", w=ROW)
        qT = arena[:, N:2 * N]
        v_rows = arena[:, 2 * N:3 * N].rearrange("p (t c) -> p t c", c=C)
        adj0 = N + REC
        adj_buf = [arena[:, adj0 + b * HALF:adj0 + (b + 1) * HALF] for b in range(NBUF)]
        y_rows = arena[:, adj0 + N:].rearrange("p (t w) -> p t w", w=YW)
        scores = arena[:, adj0 + N:adj0 + 2 * N]
        free_at = [0]

        def carve(words):
            free_at[0] += words
            return arena[:, free_at[0] - words:free_at[0]]

        KMAX = SLOTS[0]
        drawn_y = [carve(SLOTS[b] * YW) for b in range(2)]
        match = carve(KMAX * NCAND)
        assert free_at[0] <= N
        free_at[0] = adj0
        y_prod = [carve(SLOTS[b] * C) for b in range(2)]
        assert free_at[0] <= adj0 + N
        free_at[0] = 0
        drawn_kv = [carve((SLOTS[b] + 1) * 2 * C) for b in range(RING)]
        qk_prod = carve((KMAX + 1) * C)
        ev_prod = [carve((SLOTS[b] + 1) * C) for b in range(RING)]
        summed = carve(N).rearrange("p (t c) -> p t c", c=C)
        free_at[0] = max(free_at[0], adj0 + N)
        ranks_all = carve(WIDE0[T]).bitcast(U32)
        lower_all = carve(WIDE0[T])
        xsqkv = [carve(5 * C) for b in range(4)]
        rows_in = [carve(4 * C) for b in range(RING)]
        att = carve(C)
        logits = carve((KMAX + 1) * H)
        assert free_at[0] <= 3 * N + REC

        ident = sb("ident", [P, P])
        mass_sb = sb("mass_sb", [P, T])
        time_col = sb("time_col", [P, 2])
        neg_time = sb("neg_time", [P, 2])
        ev0 = sb("ev0", [P, V0])
        ev1 = sb("ev1", [P, V1])
        decay0 = sb("decay0", [P, V0])
        decay1 = sb("decay1", [P, V1])
        W_all = sb("W_all", [P, 4 * C])
        b_all = sb("b_all", [P, 4 * C])
        bq_col = sb("bq_col", [P, 1])
        bk_col = sb("bk_col", [P, 1])
        Wb_rows = sb("Wb_rows", [P, 3 * C])
        xm = [sb(f"xm{b}", [P, C]) for b in range(NBUF)]
        minus_half = sb("minus_half", [P, T])
        x_tile = sb("x_tile", [P, C])
        pre = sb("pre", [P, C])
        kept = sb("kept", [P, 2 * C])
        x1T = sb("x1T", [P, C])
        centred = sb("centred", [P, C])
        squares = sb("squares", [P, C])
        moments = sb("moments", [P, 2])
        rstd = sb("rstd", [P, 1])
        qz = sb("qz", [P, H, P])
        rowmax = sb("rowmax", [P, H])
        shift = sb("shift", [P, H])
        den = sb("den", [P, H])
        inv = sb("inv", [P, H])
        cat = sb("cat", [P, 3 * C])
        prod = sb("prod", [P, 3 * C])
        beta = sb("beta", [P, 4])
        res = sb("res", [P, C])
        kept_in = sb("kept_in", [P, 2 * C])

        junk_words = [sb(f"junk{b}", [P, HALF // 2]) for b in range(2)]
        junk = [words[:].bitcast(BF16) for words in junk_words]
        turned = [junk_words[0][:, b * BANK:(b + 1) * BANK] for b in range(2)]
        cand_val = [sb(f"cand_val{b}", [P, SEGS * 8]) for b in range(NBUF)]
        cand_col = [sb(f"cand_col{b}", [P, SEGS * 8], U32) for b in range(NBUF)]
        seg_start = [sb(f"seg_start{h}", [P, SEGS * 8]) for h in range(2)]
        cand_float = sb("cand_float", [P, SEGS * 8])
        n_pos = sb("n_pos", [P, 2, T])
        n_neg = sb("n_neg", [P, 2, T])
        tri = sb("tri", [P, P], BF16)
        ones = sb("ones", [P, P], BF16)
        cls = sb("cls", [P, NCLS])
        limit = sb("limit", [P, NCLS])
        degree = sb("degree", [P, T])
        clipped = sb("clipped", [P, T])
        rank = sb("rank", [P, T])
        rank_u = sb("rank_u", [P, T], U32)
        bad = sb("bad", [P, 8])
        bad_cls = sb("bad_cls", [P, NCLS])
        bad_sum = sb("bad_sum", [P, 1])
        bad_bf = sb("bad_bf", [P, 1], BF16)
        flag = sb("flag", [1, 1], I32)
        iota_i = sb("iota_i", [P, T], I32)
        id_all = sb("id_all", [P, T], U32)
        codes = [sb(f"codes{b}", [P, NCAND]) for b in range(3)]
        top = sb("top", [P, 32])
        draw_cols = [sb(f"draw_cols{b}", [P, KMAX], U32) for b in range(2)]
        weight = [sb(f"weight{b}", [P, KMAX]) for b in range(2)]
        stats = sb("stats", [P, 6])
        mom = sb("mom", [P, 2])
        root = sb("root", [P, 1])
        mean_var = [sb(f"mean_var{b}", [P, 2]) for b in range(RING)]
        eps_pair = sb("eps_pair", [P, 2])
        mean_var_all = sb("mean_var_all", [P, T, 2])
        minus_mean_all = sb("minus_mean_all", [P, T])
        inv_root_all = sb("inv_root_all", [P, T])
        eps_col = sb("eps_col", [P, 1])
        draw_ranks = [sb(f"draw_ranks{b}", [P, KMAX], U32) for b in range(RING)]
        diag = sb("diag", [P, T])
        small = sb("small", [P, 24])
        NHOT = NCLS * T
        hot = junk[1][:, 0:NHOT]
        up = arena[:, adj0:adj0 + NHOT]
        place = arena[:, adj0 + NHOT:adj0 + 2 * NHOT]
        no_rows = sb("no_rows", [P, BANK], BF16)

        bank = [ctx.enter_context(nc.psum_tensor(f"bank{b}", [P, BANK], F32)) for b in range(8)]

        loaded = sem("loaded")
        ident_ready = sem("ident_ready")
        adj_landed = [sem(f"adj_landed{b}") for b in range(NBUF)]
        xm_ready = sem("xm_ready")
        adj_summed = sem("adj_summed")
        decay_ready = sem("decay_ready")
        neg_ready = sem("neg_ready")
        y_scaled = sem("y_scaled")
        y_turned = [sem(f"y_turned{b}") for b in range(2)]
        y_copied = [sem(f"y_copied{b}") for b in range(2)]
        dve_step = sem("dve_step")
        block_landed = [sem(f"block_landed{b}") for b in range(2)]
        x_landed = sem("x_landed")
        turned_psum = [sem(f"turned_psum{b}") for b in range(2)]
        turned_sbuf = [sem(f"turned_sbuf{b}") for b in range(2)]
        turned_used = [sem(f"turned_used{b}") for b in range(2)]
        var_ready = sem("var_ready")
        rstd_ready = sem("rstd_ready")
        x1_ready = sem("x1_ready")
        x1T_psum = sem("x1T_psum")
        x1T_ready = sem("x1T_ready")
        proj_ready = sem("proj_ready")
        kept_ready = sem("kept_ready")
        kept_stored = sem("kept_stored")
        kept_back = sem("kept_back")
        q_ready = sem("q_ready")
        s_psum = [sem(f"s_psum{b}") for b in range(2)]
        s_masked = [sem(f"s_masked{b}") for b in range(2)]
        shift_ready = sem("shift_ready")
        exp_ready = sem("exp_ready")
        p_psum = [sem(f"p_psum{b}") for b in range(2)]
        p_sbuf = [sem(f"p_sbuf{b}") for b in range(2)]
        p_used = [sem(f"p_used{b}") for b in range(2)]
        head_used = sem("head_used")
        inv_ready = sem("inv_ready")
        logit_ready = sem("logit_ready")
        beta_ready = sem("beta_ready")
        var2_ready = sem("var2_ready")
        rstd2_ready = sem("rstd2_ready")
        res_ready = sem("res_ready")
        res_stored = sem("res_stored")
        N_CONST = 14
        N_READY = 2 * SEGS + 6 + 2 * NCLS
        carried = sem("carried")
        carried_pool = sem("carried_pool")
        carried_sp = sem("carried_sp")
        cand_max = sem("cand_max")
        cand_ready = sem("cand_ready")
        cand_used = sem("cand_used")
        counted = sem("counted")
        const_ready = sem("const_ready")
        pool_step = sem("pool_step")
        hot_ready = sem("hot_ready")
        before_ready = sem("before_ready")
        candidates_counted = sem("candidates_counted")
        rank_ready = sem("rank_ready")
        bad_ready = sem("bad_ready")
        bad_psum = sem("bad_psum")
        flag_ready = sem("flag_ready")
        y_stored = sem("y_stored")
        sorted_out = sem("sorted_out")
        record_back = sem("record_back")
        fast_step = sem("fast_step")
        draw_ready = sem("draw_ready")
        drawn = [sem(f"drawn{b}") for b in range(2)]
        drawn_used = sem("drawn_used")
        pre_ready = sem("pre_ready")
        att_ready = sem("att_ready")
        mean_ready = sem("mean_ready")
        root_ready = sem("root_ready")
        row_ready = sem("row_ready")
        rowT_psum = sem("rowT_psum")
        rowT_ready = sem("rowT_ready")
        lin_ready = sem("lin_ready")
        lin_used = sem("lin_used")
        xsq_stored = [sem(f"xsq_stored{b}") for b in range(2)]
        kv_stored = [sem(f"kv_stored{b}") for b in range(2)]
        x_loaded = sem("x_loaded")
        x_rest_loaded = sem("x_rest_loaded")
        y_half = sem("y_half")
        diag_loaded = sem("diag_loaded")
        own_added = sem("own_added")
        xsq_back = [sem(f"xsq_back{b}") for b in range(RING)]
        own_back = [sem(f"own_back{b}") for b in range(RING)]
        ranks_back = [sem(f"ranks_back{b}") for b in range(RING)]
        drawn2 = [sem(f"drawn2{b}") for b in range(RING)]
        drawn2_used = sem("drawn2_used")
        arg_ready = sem("arg_ready")
        e_ready = sem("e_ready")
        z_ready = sem("z_ready")
        aggregated = sem("aggregated")
        ez_ready = sem("ez_ready")
        blended = sem("blended")
        scale_step = sem("scale_step")
        power_ready = sem("power_ready")
        final_ready = sem("final_ready")
        final_stored = sem("final_stored")


        def gather(pool, table, cols, s, to, done):
            pool.indirect_dma_start(out=to, out_offset=None, in_=table,
                                    in_offset=bass.IndirectOffsetOnAxis(ap=cols[:, s:s + 1], axis=0)).then_inc(done, 16)

        def scatter(pool, table, ids, of, done):
            pool.indirect_dma_start(out=table, out_offset=bass.IndirectOffsetOnAxis(ap=ids, axis=0), in_=of,
                                    in_offset=None).then_inc(done, 16)


        def dense_sync(sp):
            sp.wait_ge(adj_summed, 2 * T)
            with sp.Fori(0, T) as t:
                for half in range(2):
                    sp.wait_ge(turned_psum[1], (t * 8 + 4 * half - 4 if half else t * 8) + CREDIT)
                    sp.dma_start(adj_buf[half], adj[bass.ds(t * P, P), half * HALF:(half + 1) * HALF])\
                      .then_inc(block_landed[half], 16)
                sp.wait_ge(x1_ready, t + CREDIT)
                sp.dma_start(x_tile[:], x[bass.ds(t * P, P), :]).then_inc(x_landed, 16)
                sp.wait_ge(kept_ready, t + 1 + CREDIT)
                sp.dma_start(keep[bass.ds(t * P, P), :], kept[:]).then_inc(kept_stored, 16)
            sp.wait_ge(kept_stored, 16 * T + CREDIT)
            with sp.Fori(0, T) as t:
                sp.wait_ge(s_masked[0], t * (H * 8) + CREDIT)
                sp.wait_ge(s_masked[1], t * (H * 8) + CREDIT)
                for half in range(2):
                    sp.dma_start(adj_buf[half], adj[bass.ds(t * P, P), half * HALF:(half + 1) * HALF])\
                      .then_inc(block_landed[half], 16)
                sp.wait_ge(res_ready, t + CREDIT)
                sp.dma_start(kept_in[:], keep[bass.ds(t * P, P), :]).then_inc(kept_back, 16)
                sp.wait_ge(res_ready, t + 1 + CREDIT)
                sp.dma_start(out[bass.ds(t * P, P), :], res[:]).then_inc(res_stored, 16)
            sp.wait_ge(res_stored, 16 * T + CREDIT)

        def dense_pool(pool):
            with pool.Fori(0, T) as t:
                pool.wait_ge(var_ready, t + 1)
                pool.tensor_tensor(rstd[:], moments[:, 1:2], minus_half[:, 0:1], ALU.pow).then_inc(rstd_ready, 1)
            with pool.Fori(0, T) as t:
                pool.wait_ge(var2_ready, t + 1)
                pool.tensor_tensor(rstd[:], moments[:, 1:2], minus_half[:, 0:1], ALU.pow).then_inc(rstd2_ready, 1)

        def dense_scalar(act):
            with act.Fori(0, T) as t:
                for j in range(8):
                    act.wait_ge(turned_psum[1], t * 8 + (j + 1) + CREDIT)
                    act.wait_ge(turned_used[1], t * 8 + j + CREDIT)
                    act.activation(turned[1], bank[1][:], ACT.Copy).then_inc(turned_sbuf[1], 1)
                act.wait_ge(x1T_psum, t + 1)
                act.activation(x1T[:], bank[4][:, 0:P], ACT.Copy).then_inc(x1T_ready, 1)
            with act.Fori(0, T) as t:
                for h in range(H):
                    act.wait_ge(shift_ready, t * H + (h + 1))
                    act.activation(scores, scores, ACT.Exp, bias=shift[:, h:h + 1],
                                   accum_out=den[:, h:h + 1]).then_inc(exp_ready, 1)
                    for j in range(8):
                        act.wait_ge(p_psum[1], (t * H + h) * 8 + (j + 1) + CREDIT)
                        act.wait_ge(p_used[1], (t * H + h) * 8 + j + CREDIT)
                        act.activation(turned[1], bank[1][:], ACT.Copy).then_inc(p_sbuf[1], 1)
                act.wait_ge(logit_ready, t + 1)
                act.activation(beta[:, 1:2], beta[:, 0:1], ACT.Exp, scale=-1.0).then_inc(beta_ready, 1)

        def dense_tensor(pe):
            with pe.Fori(0, T) as t:
                def add_group(j):
                    pe.wait_ge(turned_sbuf[j % 2], t * 8 + (j // 2 + 1) + CREDIT)
                    for i in range(4):
                        m = 4 * j + i
                        mm = pe.matmul(bank[2][:, 0:C], turned[j % 2][:, i * P:(i + 1) * P], y_rows[:, m, 0:C],
                                       start=m == 0, stop=m == T - 1)
                    mm.then_inc(turned_used[j % 2], 1)
                    return mm

                for j in range(16):
                    if j % 8 == 0:
                        pe.wait_ge(block_landed[j // 8], t * 16 + 16)
                    pe.wait_ge(turned_sbuf[j % 2], t * 8 + j // 2 + CREDIT)
                    for i in range(4):
                        k = 4 * (j % 8) + i
                        tp = pe.transpose(bank[j % 2][:, i * P:(i + 1) * P],
                                          adj_buf[j // 8][:, k * P:(k + 1) * P], ident[:])
                    tp.then_inc(turned_psum[j % 2], 1)
                    if j:
                        add_group(j - 1)
                add_group(15)
                pe.wait_ge(x1_ready, t + 1 + CREDIT)
                pe.wait_ge(kept_ready, t + CREDIT)
                pe.transpose(bank[4][:, 0:P], kept[:, 0:C], ident[:]).then_inc(x1T_psum, 1)
                pe.wait_ge(x1T_ready, t + 1)
                pe.matmul(bank[5][:, 0:P], W_all[:, C:2 * C], x1T[:], start=True, stop=True)
                pe.matmul(bank[5][:, P:2 * P], W_all[:, 2 * C:3 * C], x1T[:], start=True, stop=True)
                pe.matmul(bank[5][:, 2 * P:3 * P], x1T[:], W_all[:, 3 * C:], start=True, stop=True)
                pe.matmul(bank[5][:, 3 * P:], x1T[:], W_all[:, 0:C], start=True, stop=True)\
                  .then_inc(proj_ready, 1)

            pe.wait_ge(kept_ready, T + CREDIT)
            with pe.Fori(0, T) as t:
                pe.wait_ge(q_ready, t + 1)
                for h in range(H):
                    u = t * H + h
                    for j in range(16):
                        pe.wait_ge(s_masked[j % 2], u * 8 + j // 2 + CREDIT)
                        pe.matmul(bank[6 + j % 2][:], qz[:, h, :], kT[:, j * BANK:(j + 1) * BANK],
                                  start=True, stop=True).then_inc(s_psum[j % 2], 1)

                    def add_values(j):
                        pe.wait_ge(p_sbuf[j % 2], u * 8 + (j // 2 + 1) + CREDIT)
                        for i in range(4):
                            m = 4 * j + i
                            mm = pe.matmul(bank[2][:, 0:HC], turned[j % 2][:, i * P:(i + 1) * P],
                                           v_rows[:, m, h * HC:(h + 1) * HC], start=m == 0, stop=m == T - 1)
                        mm.then_inc(p_used[j % 2], 1)
                        return mm

                    pe.wait_ge(exp_ready, u + 1)
                    for j in range(16):
                        pe.wait_ge(p_sbuf[j % 2], u * 8 + j // 2 + CREDIT)
                        for i in range(4):
                            k = 4 * j + i
                            tp = pe.transpose(bank[j % 2][:, i * P:(i + 1) * P], scores[:, k * P:(k + 1) * P],
                                              ident[:])
                        tp.then_inc(p_psum[j % 2], 1)
                        if j == 1:
                            pe.wait_ge(head_used, u + CREDIT)
                        if j:
                            add_values(j - 1)
                    add_values(15)

        def dense_vector(dve, step):
            def normalise(src, dst, asked, given, count):
                step(dve.reduce_sum(moments[:, 0:1], src, AX_X))
                step(dve.tensor_scalar(moments[:, 0:1], moments[:, 0:1], 1.0 / C, None, ALU.mult))
                step(dve.tensor_scalar(centred[:], src, moments[:, 0:1], None, ALU.subtract))
                step(dve.scalar_tensor_tensor(out=squares[:], in0=centred[:], scalar=1.0, in1=centred[:],
                                              op0=ALU.mult, op1=ALU.mult, accum_out=moments[:, 1:2]))
                dve.tensor_scalar(moments[:, 1:2], moments[:, 1:2], 1.0 / C, EPS, ALU.mult, ALU.add).then_inc(asked, 1)
                dve.wait_ge(given, count)
                return dve.tensor_scalar(dst, centred[:], rstd[:], None, ALU.mult)

            dve.wait_ge(y_stored, 16 * 4)
            dve.wait_ge(sorted_out, 16 * T)
            with dve.Fori(0, T) as t:
                step.enter(t, 5)
                for j in range(8):
                    dve.wait_ge(turned_psum[0], t * 8 + (j + 1) + CREDIT)
                    dve.wait_ge(turned_used[0], t * 8 + j + CREDIT)
                    dve.tensor_copy(turned[0], bank[0][:]).then_inc(turned_sbuf[0], 1)
                dve.wait_ge(turned_used[1], t * 8 + 8 + CREDIT)
                dve.wait_ge(x_landed, t * 16 + 16)
                step(dve.tensor_tensor(pre[:], bank[2][:, 0:C], x_tile[:], ALU.add))
                dve.wait_ge(kept_stored, t * 16 + CREDIT)
                normalise(pre[:], kept[:, 0:C], var_ready, rstd_ready, t + 1).then_inc(x1_ready, 1)
                dve.wait_ge(proj_ready, t + 1)
                dve.tensor_scalar(qT[:, bass.ds(t * P, P)], bank[5][:, 0:P], bq_col[:], None, ALU.add)
                dve.tensor_scalar(kT[:, bass.ds(t * P, P)], bank[5][:, P:2 * P], bk_col[:], None, ALU.add)
                dve.tensor_tensor(v_rows[:, t, :], bank[5][:, 2 * P:3 * P], b_all[:, 3 * C:], ALU.add)
                dve.tensor_tensor(kept[:, C:], bank[5][:, 3 * P:], b_all[:, 0:C], ALU.add).then_inc(kept_ready, 1)
                step.leave(T)

            for h in range(H):
                last = dve.memset(qz[:, h, :], 0.0)
            step(last)
            with dve.Fori(0, T) as t:
                step.enter(t, 1 + 3 * H + 10)
                for half in range(2):
                    dve.wait_ge(block_landed[half], t * 16 + 16 * (T + 1))
                    last = dve.tensor_scalar(adj_buf[half], adj_buf[half], 0.0, -FAR, ALU.is_equal, ALU.mult)
                step(last)
                for h in range(H):
                    rows = slice(h * HC, (h + 1) * HC)
                    last = dve.tensor_copy(qz[rows, h, :], qT[rows, bass.ds(t * P, P)])
                last.then_inc(q_ready, 1)
                for h in range(H):
                    u = t * H + h
                    dve.wait_ge(p_psum[0], u * 8 + CREDIT)
                    dve.wait_ge(p_psum[1], u * 8 + CREDIT)
                    for j in range(16):
                        dve.wait_ge(s_psum[j % 2], u * 8 + (j // 2 + 1))
                        dve.scalar_tensor_tensor(
                            out=scores[:, j * BANK:(j + 1) * BANK], in0=bank[6 + j % 2][:], scalar=SCALE,
                            in1=adj_buf[j // 8][:, (j % 8) * BANK:(j % 8 + 1) * BANK],
                            op0=ALU.mult, op1=ALU.add).then_inc(s_masked[j % 2], 1)
                    dve.wait_ge(s_masked[0], u * 8 + 8 + CREDIT)
                    dve.wait_ge(s_masked[1], u * 8 + 8 + CREDIT)
                    step(dve.reduce_max(rowmax[:, h:h + 1], scores, AX_X))
                    step(dve.tensor_scalar(shift[:, h:h + 1], rowmax[:, h:h + 1], -FAR / 2, -1.0, ALU.is_gt, ALU.mult))
                    dve.tensor_tensor(shift[:, h:h + 1], shift[:, h:h + 1], rowmax[:, h:h + 1], ALU.mult)\
                       .then_inc(shift_ready, 1)
                    for j in range(8):
                        dve.wait_ge(p_psum[0], u * 8 + (j + 1) + CREDIT)
                        dve.wait_ge(p_used[0], u * 8 + j + CREDIT)
                        dve.tensor_copy(turned[0], bank[0][:]).then_inc(p_sbuf[0], 1)
                    dve.wait_ge(exp_ready, u + 1)
                    step(dve.scalar_tensor_tensor(out=inv[:, h:h + 1], in0=den[:, h:h + 1], scalar=0.0,
                                                  in1=den[:, h:h + 1], op0=ALU.is_equal, op1=ALU.add))
                    dve.reciprocal(inv[:, h:h + 1], inv[:, h:h + 1]).then_inc(inv_ready, 1)
                    dve.wait_ge(inv_ready, u + 1)
                    dve.wait_ge(p_used[1], u * 8 + 8 + CREDIT)
                    dve.tensor_scalar(cat[:, 0:C].rearrange("p (c h) -> p h c", h=H)[:, h, :], bank[2][:, 0:HC],
                                      inv[:, h:h + 1], None, ALU.mult).then_inc(head_used, 1)
                dve.wait_ge(head_used, t * H + H + CREDIT)
                dve.wait_ge(kept_back, t * 16 + 16)
                dve.tensor_copy(cat[:, C:2 * C], kept_in[:, C:])
                step(dve.tensor_tensor(cat[:, 2 * C:], cat[:, 0:C], kept_in[:, C:], ALU.subtract))
                step(dve.tensor_tensor(prod[:], cat[:], Wb_rows[:], ALU.mult))
                dve.reduce_sum(beta[:, 0:1], prod[:], AX_X).then_inc(logit_ready, 1)
                dve.wait_ge(beta_ready, t + 1)
                step(dve.tensor_scalar(beta[:, 2:3], beta[:, 1:2], 1.0, None, ALU.add))
                step(dve.reciprocal(beta[:, 3:4], beta[:, 2:3]))
                step(dve.scalar_tensor_tensor(out=prod[:, 0:C], in0=cat[:, 2 * C:], scalar=beta[:, 3:4],
                                              in1=cat[:, 0:C], op0=ALU.mult, op1=ALU.subtract))
                step(dve.tensor_tensor(pre[:], kept_in[:, 0:C], prod[:, 0:C], ALU.subtract))
                dve.wait_ge(res_stored, t * 16 + CREDIT)
                normalise(pre[:], res[:], var2_ready, rstd2_ready, t + 1).then_inc(res_ready, 1)
                step.leave(T)




        def at(first, turn, ways=2):
            return first + ways * turn

        def stored(first, turn, ways=2):
            return 16 * (first // ways) + 16 * turn

        def row_buf(first):
            return xsqkv[first % 2 + (2 if first >= T - 2 else 0)]

        def gathered(first, turn, ways):
            return 16 * SLOTS[first] * turn + 16 * WAYS_SLOTS[ways][first]

        def own_and_slots(first, turn, ways):
            return bass.ds(WIDE0[first] + ways * (SLOTS[first] + 1) * turn, SLOTS[first] + 1)

        def slots_of(first, turn, ways):
            return bass.ds(WIDE0[first] + 1 + ways * (SLOTS[first] + 1) * turn, SLOTS[first])

        def carry(eng, carrier, turn):
            if not isinstance(turn, int):
                eng.sem_inc(carrier, 1)

        def closed(tiles):
            return tiles - 3

        def sparse_sync(sp):
            sp.wait_ge(sorted_out, 16 * T)
            with sp.Fori(0, T) as t:
                sp.dma_start(rec[:, t, :], records[bass.ds(t * P, P), :]).then_inc(record_back, 16)
                sp.wait_ge(record_back, t * 16 + 16)
                carry(sp, carried_sp, t)

            def load_ranks(first, turn):
                b, t = first % RING, at(first, turn, RING)
                if first >= RING:
                    sp.wait_ge(drawn2_used, t - (RING - 1))
                carry(sp, carried_sp, turn)
                sp.dma_start(draw_ranks[b][:, 0:SLOTS[first]], ranks_all[:, slots_of(first, turn, RING)])\
                  .then_inc(ranks_back[b], 16)

            def load(first, turn):
                if first >= RING:
                    load_ranks(first, turn)
                b, t = first % RING, at(first, turn, RING)
                sp.dma_start(drawn_kv[b][:, 0:2 * C], kv_table[bass.ds(t * P, P), :]).then_inc(own_back[b], 16)

            sp.wait_ge(drawn_used, RING)
            for first in range(RING):
                load_ranks(first, 0)
            for p in range(2):
                sp.wait_ge(xsq_stored[p], 16 * (T // 2))
                sp.wait_ge(kv_stored[p], 16 * (T // 2))
            for_tiles(sp, load, RING)
            sp.wait_ge(final_stored, 16 * T)

        def sparse_pool(pool):
            pool.wait_ge(y_stored, 16 * 4)

            def draw(first, turn):
                p = first % 2
                pool.wait_ge(draw_ready, at(first, turn) + 1)
                if first >= 2:
                    pool.wait_ge(drawn_used, at(first, turn) - 1)
                carry(pool, carried_pool, turn)
                for s in range(SLOTS[first]):
                    gather(pool, y_table, draw_cols[p], s, drawn_y[p][:, s * YW:(s + 1) * YW], drawn[p])

            for_tiles(pool, draw, 2)
            for p in range(2):
                pool.wait_ge(kv_stored[p], 16 * (T // 2))

            def draw2(first, turn):
                b = first % RING
                pool.wait_ge(ranks_back[b], stored(first, turn, RING) + 16)
                carry(pool, carried_pool, turn)
                for s in range(SLOTS[first]):
                    gather(pool, kv_table, draw_ranks[b], s, drawn_kv[b][:, (s + 1) * 2 * C:(s + 2) * 2 * C], drawn2[b])

            def store_out(last, now):
                for t in range(last, now):
                    scatter(pool, out, id_all[:, t:t + 1], summed[:, t, :], final_stored)

            batches = [0]

            def power(now):
                last = batches[-1]
                pool.wait_ge(blended, now)
                inv_root, shifted = inv_root_all[:, last:now], minus_mean_all[:, last:now]
                pool.tensor_tensor(inv_root, mean_var_all[:, last:now, 1], minus_half[:, last:now], ALU.pow)\
                    .then_inc(scale_step, 1)
                n = 2 * len(batches)
                pool.wait_ge(scale_step, n - 1)
                pool.tensor_tensor(shifted, mean_var_all[:, last:now, 0], inv_root, ALU.mult).then_inc(scale_step, 1)
                pool.wait_ge(scale_step, n)
                pool.tensor_scalar(shifted, shifted, -1.0, None, ALU.mult).then_inc(power_ready, 1)
                batches.append(now)

            def close_batch(tiles):
                if closed(tiles) > batches[-1]:
                    if len(batches) > 1:
                        pool.wait_ge(final_ready, len(batches) - 1)
                        store_out(batches[-2], batches[-1])
                    power(closed(tiles))

            for_tiles(pool, draw2, RING, after=close_batch)
            pool.wait_ge(final_ready, len(batches) - 1)
            store_out(batches[-2], batches[-1])
            power(T)
            pool.wait_ge(final_ready, len(batches) - 1)
            store_out(batches[-2], batches[-1])

        def sparse_scalar(act):
            def store_xsq(first, turn):
                p, t = first % 2, at(first, turn)
                act.wait_ge(lin_used, t + 1)
                rows = bass.ds(t * P, P)
                act.dma_start(kv_table[rows, :], row_buf(first)[:, 3 * C:]).then_inc(kv_stored[p], 16)
                act.dma_start(xsq_rows[rows, :], row_buf(first)[:, 0:3 * C]).then_inc(xsq_stored[p], 16)

            def layer0(first, turn):
                t = at(first, turn)
                act.wait_ge(mean_ready, t + 1)
                act.activation(root[:], mom[:, 1:2], ACT.Sqrt, bias=eps_col[:]).then_inc(root_ready, 1)
                act.wait_ge(rowT_psum, t + 1)
                act.activation(x1T[:], bank[4][:, 0:P], ACT.Copy).then_inc(rowT_ready, 1)
                if first >= 1:
                    store_xsq(first - 1, turn)

            for_tiles(act, layer0, 2)
            store_xsq(T - 1, 0)

            def exp_z(first, turn):
                act.wait_ge(z_ready, at(first, turn, RING) + 1)
                act.activation(small[:, 20:21], small[:, 16:17], ACT.Exp, scale=-1.0).then_inc(ez_ready, 1)

            def load_rows(first, turn):
                b, t = first % RING, at(first, turn, RING)
                act.dma_start(rows_in[b][:, C:], xsq_rows[bass.ds(t * P, P), :]).then_inc(xsq_back[b], 16)

            def layer1(first, turn):
                if first >= 1:
                    exp_z(first - 1, turn)
                act.wait_ge(arg_ready, at(first, turn, RING) + 1)
                e = logits[:, 0:(SLOTS[first] + 1) * H]
                act.activation(e, e, ACT.Exp).then_inc(e_ready, 1)
                if first + 1 < T:
                    load_rows(first + 1, turn)

            for p in range(2):
                act.wait_ge(xsq_stored[p], 16 * (T // 2))
            load_rows(0, 0)

            batches = [0]

            def finish(tiles):
                if tiles > batches[-1]:
                    act.wait_ge(power_ready, len(batches))
                    for t in range(batches[-1], tiles):
                        last = act.activation(summed[:, t, :], summed[:, t, :], ACT.Identity,
                                              scale=inv_root_all[:, t:t + 1], bias=minus_mean_all[:, t:t + 1])
                    last.then_inc(final_ready, 1)
                    batches.append(tiles)

            for_tiles(act, layer1, RING, after=lambda tiles: finish(closed(tiles)))
            exp_z(T - 1, 0)
            finish(T)

        def sparse_tensor(pe):
            def layer0(first, turn):
                p, t = first % 2, at(first, turn)
                pe.wait_ge(drawn_used, t + 1)
                for s in range(SLOTS[first]):
                    pe.matmul(bank[p][:, 0:C], ident[:], y_prod[p][:, s * C:(s + 1) * C], start=s == 0, stop=False)
                pe.matmul(bank[p][:, 0:C], ident[:], rec[:, t, 0:C], start=False, stop=True).then_inc(pre_ready, 1)
                if first >= 1:
                    linear(first - 1, turn)

            def linear(first, turn):
                p, t = first % 2, at(first, turn)
                pe.wait_ge(row_ready, t + 1)
                pe.transpose(bank[4][:, 0:P], row_buf(first)[:, 2 * C:3 * C], ident[:]).then_inc(rowT_psum, 1)
                pe.wait_ge(rowT_ready, t + 1)
                pe.matmul(bank[6 + p][:], x1T[:], W_all[:], start=True, stop=True).then_inc(lin_ready, 1)

            for_tiles(pe, layer0, 2)
            linear(T - 1, 0)

            def layer1(first, turn):
                b = first % RING
                pe.wait_ge(drawn2_used, at(first, turn, RING) + 1)
                for s in range(SLOTS[first] + 1):
                    mm = pe.matmul(bank[b][:, 0:C], ident[:], ev_prod[b][:, s * C:(s + 1) * C], start=s == 0,
                                   stop=s == SLOTS[first])
                mm.then_inc(att_ready, 1)

            for_tiles(pe, layer1, RING)

        def sparse_vector(dve):
            step = Steps(dve, fast_step, carried)

            def wide(ap, n):
                return ap.unsqueeze(2).to_broadcast([P, ap.shape[1], n])

            def over(ap, n):
                return ap.unsqueeze(1).to_broadcast([P, n, ap.shape[1]])

            def choose(first, turn):
                p, t, K = first % 2, at(first, turn), SLOTS[first]
                rounds = -(-K // 8)
                dve.wait_ge(record_back, t * 16 + 16)
                step(dve.scalar_tensor_tensor(out=codes[0][:], in0=rec[:, t, AT_VAL:AT_VAL + NCAND], scalar=0.0,
                                              in1=rec[:, t, AT_COL:AT_COL + NCAND], op0=ALU.is_gt, op1=ALU.mult))
                step(dve.scalar_tensor_tensor(out=codes[0][:], in0=rec[:, t, AT_COL:AT_COL + NCAND],
                                              scalar=rec[:, t, AT_ID + 1:AT_ID + 2], in1=codes[0][:],
                                              op0=ALU.not_equal, op1=ALU.mult), True)
                held = codes[0]
                for r in range(rounds):
                    eight = top[:, 8 * r:8 * r + 8]
                    step(dve.max(eight, held[:]), r + 1 < rounds)
                    if r + 1 < rounds:
                        rest = codes[1 + r % 2]
                        step(dve.match_replace(rest[:], eight, held[:], 0.0), True)
                        held = rest
                dve.tensor_scalar(draw_cols[p][:, 0:K], top[:, 0:K], 1.0, 0.0, ALU.subtract, ALU.max)\
                   .then_inc(draw_ready, 1)

            def look_up(first, turn):
                p, t, K = first % 2, at(first, turn), SLOTS[first]
                same = match[:, 0:K * NCAND].rearrange("p (s c) -> p s c", c=NCAND)
                at_slots = slots_of(first, turn, 2)
                dve.tensor_scalar(lower_all[:, at_slots], top[:, 0:K], 0.0, -FAR, ALU.is_equal, ALU.mult)
                dve.tensor_copy(id_all[:, bass.ds(t, 1)], rec[:, t, AT_ID:AT_ID + 1])
                step(dve.tensor_tensor(same, wide(top[:, 0:K], NCAND), over(codes[0][:], K), ALU.is_equal))
                step(dve.tensor_tensor(same, same, over(rec[:, t, AT_VAL:AT_VAL + NCAND], K), ALU.mult))
                dve.tensor_reduce(weight[p][:, 0:K], same, AX_X, ALU.add)

            def weigh_y(first, turn):
                p, t, K = first % 2, at(first, turn), SLOTS[first]
                dve.wait_ge(drawn[p], gathered(first, turn, 2))
                rows = drawn_y[p][:, 0:K * YW].rearrange("p (s w) -> p s w", w=YW)
                dve.tensor_copy(ranks_all[:, slots_of(first, turn, 2)], rows[:, :, C])
                dve.tensor_tensor(y_prod[p][:, 0:K * C].rearrange("p (s c) -> p s c", c=C), rows[:, :, 0:C],
                                  wide(weight[p][:, 0:K], C), ALU.mult).then_inc(drawn_used, 1)

            def measure(first, turn):
                dve.wait_ge(pre_ready, at(first, turn) + 1)
                carry(dve, carried, turn)
                step(dve.bn_stats(stats[:], bank[first % 2][:, 0:C]), True)
                dve.bn_aggr(mom[:], stats[:]).then_inc(mean_ready, 1)

            def take_lin(first, turn):
                p, t = first % 2, at(first, turn)
                dve.wait_ge(lin_ready, t + 1)
                if 2 <= first < T - 2:
                    dve.wait_ge(kv_stored[p], stored(first, turn))
                dve.tensor_tensor(row_buf(first).rearrange("p (a c) -> p a c", c=C)[:, 0:2, :],
                                  bank[6 + p][:, 0:2 * C].rearrange("p (a c) -> p a c", c=C),
                                  b_all[:, 0:2 * C].rearrange("p (a c) -> p a c", c=C), ALU.add)
                dve.tensor_tensor(row_buf(first)[:, 3 * C:], bank[6 + p][:, 2 * C:], b_all[:, 2 * C:], ALU.add)\
                   .then_inc(lin_used, 1)

            def normalise_x1(first, turn):
                p, t = first % 2, at(first, turn)
                dve.wait_ge(root_ready, t + 1)
                if 2 <= first < T - 2:
                    dve.wait_ge(xsq_stored[p], stored(first, turn))
                step(dve.reciprocal(rstd[:], root[:]))
                dve.tensor_scalar(row_buf(first)[:, 2 * C:3 * C], bank[p][:, 0:C], mom[:, 0:1], rstd[:], ALU.subtract, ALU.mult)\
                   .then_inc(row_ready, 1)

            def layer0(first, turn):
                weigh_y(first, turn)
                if first >= 1:
                    measure(first - 1, turn)
                if first + 2 < T:
                    choose(first + 2, turn)
                if first >= 1:
                    normalise_x1(first - 1, turn)
                if first >= 2:
                    take_lin(first - 2, turn)
                if first + 2 < T:
                    look_up(first + 2, turn)

            dve.wait_ge(y_stored, 16 * 4)
            dve.wait_ge(own_added, T)
            step(dve.memset(lower_all, 0.0))
            for t in range(2):
                choose(t, 0)
                look_up(t, 0)
            for_tiles(dve, layer0, 2, step, lambda first: 5 + 2 * -(-SLOTS[first + 2] // 8))
            measure(T - 1, 0)
            normalise_x1(T - 1, 0)
            take_lin(T - 2, 0)
            take_lin(T - 1, 0)

            def layer1(first, turn):
                b, t, K = first % RING, at(first, turn, RING), SLOTS[first] + 1
                gated, blended_now = first >= 1, first >= 2
                dve.wait_ge(drawn2[b], gathered(first, turn, RING))
                dve.wait_ge(xsq_back[b], stored(first, turn, RING) + 16)
                dve.wait_ge(own_back[b], stored(first, turn, RING) + 16)
                kv = drawn_kv[b][:, 0:K * 2 * C].rearrange("p (s c) -> p s c", c=2 * C)
                qk = qk_prod[:, 0:K * C]
                lg = logits[:, 0:K * H]
                lg3 = lg.rearrange("p (s h) -> p s h", h=H)
                lgT = lg.rearrange("p (s h) -> p h s", h=H)
                multiplied = step.mark(dve.tensor_tensor(
                    qk.rearrange("p (s c) -> p s c", c=C), kv[:, :, 0:C], over(rows_in[b][:, 2 * C:3 * C], K), ALU.mult))
                if blended_now:
                    one_more = add_one(t - 2)
                step.need(multiplied)
                dotted = step.mark(dve.tensor_reduce(lg, qk.rearrange("p (x c) -> p x c", c=HC), AX_X, ALU.add))
                if blended_now:
                    step.need(one_more)
                    inverted = invert()
                if gated:
                    scaled = scale_out(first - 1, turn)
                if blended_now:
                    step.need(inverted)
                    mixed = mix(first - 2)
                step.need(dotted)
                masked = step.mark(dve.scalar_tensor_tensor(
                    out=lg3, in0=lg3, scalar=SCALE, in1=wide(lower_all[:, own_and_slots(first, turn, RING)], H),
                    op0=ALU.mult, op1=ALU.add))
                if gated:
                    step.need(scaled)
                    less = take_off(first - 1)
                step.need(masked)
                most = step.mark(dve.tensor_reduce(small[:, 0:H], lgT, AX_X, ALU.max))
                if blended_now:
                    step.need(mixed)
                    whole = add_x1(first - 2, turn)
                step.need(most)
                dve.tensor_tensor(lg3, lg3, over(small[:, 0:H], K), ALU.subtract).then_inc(arg_ready, 1)
                if gated:
                    step.need(less)
                    sum_z(first - 1)
                if blended_now:
                    step.need(whole)
                    spread = measure_out(first - 2, turn)
                dve.wait_ge(e_ready, t + 1)
                dve.tensor_tensor(
                    ev_prod[b][:, 0:K * C].rearrange("p (s h c) -> p s h c", h=H, c=HC),
                    kv[:, :, C:].rearrange("p s (h c) -> p s h c", c=HC),
                    lg3.unsqueeze(3).to_broadcast([P, K, H, HC]), ALU.mult).then_inc(drawn2_used, 1)
                total = step.mark(dve.tensor_reduce(small[:, 4:8], lgT, AX_X, ALU.add))
                if blended_now:
                    step.need(spread)
                    aggregate(first - 2, turn)
                step.need(total)
                dve.reciprocal(small[:, 12:16], small[:, 4:8]).then_inc(inv_ready, 1)
                if blended_now:
                    add_eps(first - 2, turn)

            def add_one(t):
                dve.wait_ge(ez_ready, t + 1)
                return step.mark(dve.tensor_scalar(small[:, 21:22], small[:, 20:21], 1.0, None, ALU.add))

            def invert():
                return step.mark(dve.reciprocal(small[:, 22:23], small[:, 21:22]))

            def scale_out(first, turn):
                b, t = first % RING, at(first, turn, RING)
                dve.wait_ge(inv_ready, t + 1)
                dve.wait_ge(att_ready, t + 1)
                return step.mark(dve.tensor_tensor(rows_in[b][:, 0:C].rearrange("p (c h) -> p h c", h=H),
                                                   bank[b][:, 0:C].rearrange("p (h c) -> p h c", h=H),
                                                   wide(small[:, 12:16], HC), ALU.mult))

            def take_off(first):
                rows = rows_in[first % RING]
                return step.mark(dve.tensor_tensor(rows[:, 2 * C:3 * C], rows[:, 0:C], rows[:, C:2 * C], ALU.subtract))

            def sum_z(first):
                dve.scalar_tensor_tensor(out=cat[:], in0=rows_in[first % RING][:, 0:3 * C], scalar=1.0, in1=Wb_rows[:],
                                         op0=ALU.mult, op1=ALU.mult, accum_out=small[:, 16:17]).then_inc(z_ready, 1)

            def mix(first):
                rows = rows_in[first % RING]
                return step.mark(dve.scalar_tensor_tensor(out=att, in0=rows[:, 2 * C:3 * C], scalar=small[:, 22:23],
                                                          in1=rows[:, 0:C], op0=ALU.mult, op1=ALU.subtract))

            def add_x1(first, turn):
                b = first % RING
                return step.mark(dve.tensor_tensor(summed[:, at(first, turn, RING), :], rows_in[b][:, 3 * C:], att,
                                                   ALU.subtract))

            def measure_out(first, turn):
                carry(dve, carried, turn)
                return step.mark(dve.bn_stats(stats[:], summed[:, at(first, turn, RING), :]))

            def aggregate(first, turn):
                carry(dve, carried, turn)
                dve.bn_aggr(mean_var[first % RING][:], stats[:]).then_inc(aggregated, 1)

            def add_eps(first, turn):
                t = at(first, turn, RING)
                dve.wait_ge(aggregated, t + 1)
                dve.tensor_tensor(mean_var_all[:, t, :], mean_var[first % RING][:], eps_pair[:], ALU.add)\
                   .then_inc(blended, 1)

            def close(gate, blend):
                if gate is not None:
                    step.need(scale_out(gate, 0))
                    step.need(take_off(gate))
                step.need(add_one(blend))
                if gate is not None:
                    sum_z(gate)
                step.need(invert())
                step.need(mix(blend))
                step.need(add_x1(blend, 0))
                step.need(measure_out(blend, 0))
                aggregate(blend, 0)
                add_eps(blend, 0)

            for_tiles(dve, layer1, RING, step, lambda first: 12)
            close(T - 1, T - 2)
            close(None, T - 1)



        block = ctx.enter_context(nc.Block())

        @block.sync
        def _(sp):
            def load_block(h, g, b):
                rows = bass.ds((g * NBUF + b) * P, P)
                sp.dma_start(adj_buf[b], adj[rows, h * HALF:(h + 1) * HALF]).then_inc(adj_landed[b], 16)

            load_block(0, 0, 0)
            x_tiles = x.rearrange("(t p) c -> p t c", p=P)
            sp.dma_start(mass_sb[:], mass).then_inc(x_loaded, 16)
            sp.dma_start(rec[:, 0:NBUF, 0:C], x_tiles[:, 0:NBUF, :]).then_inc(x_loaded, 16)
            for b in (1, 2):
                load_block(0, 0, b)
            for to, of in (
                (time_col[:], diff_time),
                (ev0[:], evals0.partition_broadcast(P)),
                (ev1[:], evals1.partition_broadcast(P)),
                (W_all[:, 0:C], Ws), (W_all[:, C:2 * C], Wq), (W_all[:, 2 * C:3 * C], Wk), (W_all[:, 3 * C:], Wv),
                (b_all[:, 0:C], bs.partition_broadcast(P)), (b_all[:, C:2 * C], bq_row.partition_broadcast(P)),
                (b_all[:, 2 * C:3 * C], bk_row.partition_broadcast(P)), (b_all[:, 3 * C:], bv.partition_broadcast(P)),
                (bq_col[:], bq), (bk_col[:], bk),
                (Wb_rows[:], Wb.rearrange("c a -> (a c)").partition_broadcast(P)),
            ):
                sp.dma_start(to, of).then_inc(loaded, 16)
            sp.dma_start(rec[:, NBUF:, 0:C], x_tiles[:, NBUF:, :]).then_inc(x_rest_loaded, 16)
            for b in range(3, NBUF):
                load_block(0, 0, b)
            sp.dma_start(diag[:], adj.rearrange("a b -> (a b)")[0:N * N:N + 1].rearrange("(t p) -> p t", p=P),
                         allow_slow_non_contiguous=True).then_inc(diag_loaded, 16)
            for h in range(2):
                with sp.Fori(1 - h, T // NBUF) as g:
                    for b in range(NBUF):
                        past = h * T + g * NBUF + (b + 1 - NBUF)
                        sp.wait_ge(adj_summed, past)
                        sp.wait_ge(cand_ready, past)
                        sp.wait_ge(counted, past)
                        load_block(h, g, b)

            sp.wait_ge(y_copied[0], 8)
            sp.wait_ge(y_copied[1], 8)
            sp.wait_ge(rank_ready, 1)
            for part in range(4):
                tiles = slice(part * T // 4, (part + 1) * T // 4)
                sp.dma_start(y_table[part * N // 4:(part + 1) * N // 4, :].rearrange("(t p) c -> p t c", p=P),
                             y_rows[:, tiles, :]).then_inc(y_stored, 16)
            sp.wait_ge(flag_ready, 1)
            dense = sp.value_load(flag[0:1, 0:1], min_val=0, max_val=1)
            with sp.If(dense):
                dense_sync(sp)
            with sp.Else():
                sparse_sync(sp)

        @block.gpsimd
        def _(pool):
            for credited in (*turned_psum, *turned_sbuf, *turned_used, x1_ready, kept_ready, kept_stored, *s_masked,
                             res_ready, *p_psum, *p_sbuf, *p_used, head_used, res_stored):
                pool.sem_inc(credited, CREDIT)
            pool.memset(ident[:], 0.0).then_inc(ident_ready, 1)
            pool.memset(minus_half[:], -0.5).then_inc(ident_ready, 1)
            pool.wait_ge(ident_ready, 2)
            pool.affine_select(out=ident[:], in_=ident[:], compare_op=ALU.not_equal, fill=1.0, base=0,
                               pattern=[[-1, P]], channel_multiplier=1).then_inc(ident_ready, 1)
            step = Steps(pool, pool_step, carried_pool)
            for h in range(2):
                for k in range(SEGS):
                    pool.memset(seg_start[h][:, 8 * k:8 * k + 8], float(h * HALF + k * SEG + 1)).then_inc(const_ready, 1)
            pool.memset(ones[:], 1.0).then_inc(const_ready, 1)
            pool.memset(no_rows[:], 0.0).then_inc(const_ready, 1)
            pool.memset(eps_col[:], EPS).then_inc(const_ready, 1)
            pool.memset(eps_pair[:, 0:1], 0.0).then_inc(const_ready, 1)
            pool.memset(eps_pair[:, 1:2], EPS).then_inc(const_ready, 1)
            step(pool.memset(tri[:], 1.0))
            pool.affine_select(out=tri[:], in_=tri[:], compare_op=ALU.is_gt, fill=0.0, base=0,
                               pattern=[[1, P]], channel_multiplier=-1).then_inc(const_ready, 1)
            for k in range(NCLS):
                pool.memset(cls[:, k:k + 1], float(MOST - k)).then_inc(const_ready, 1)
                fit = sum(n + 1 >= (MOST - k if k else SLOTS[0] + 1) for n in SLOTS) if k < NCLS - 1 else T
                pool.memset(limit[:, k:k + 1], float(fit * P)).then_inc(const_ready, 1)
            step(pool.iota(iota_i[:], [[P, T]], base=0, channel_multiplier=1))
            step(pool.tensor_copy(rec[:, :, AT_ID:AT_ID + 1].rearrange("p t a -> p (t a)"), iota_i[:]))
            step(pool.tensor_scalar(iota_i[:], iota_i[:], 1, None, ALU.add))
            step(pool.tensor_copy(rec[:, :, AT_ID + 1:AT_ID + 2].rearrange("p t a -> p (t a)"), iota_i[:]))
            step(pool.memset(rec[:, :, AT_ID + 2:ROW], 0.0))
            pool.wait_ge(const_ready, N_READY)

            def file(h, g, b):
                t = g * NBUF + b
                pool.wait_ge(cand_ready, g * NBUF + (h * T + b + 1))
                pool.sem_inc(carried_pool, 1)
                at = h * SEGS * 8
                step(pool.tensor_copy(cand_float[:], cand_col[b][:]))
                step(pool.tensor_tensor(rec[:, t, AT_COL + at:AT_COL + at + SEGS * 8], cand_float[:], seg_start[h][:],
                                        ALU.add))
                pool.tensor_copy(rec[:, t, AT_VAL + at:AT_VAL + at + SEGS * 8], cand_val[b][:]).then_inc(cand_used, 1)

            for h in range(2):
                if h:
                    half_y = yT[:, 0:HALF].rearrange("p (t v) -> p t v", v=V1)
                    pool.wait_ge(y_scaled, 8)
                    pool.tensor_tensor(half_y, half_y, decay1[:].unsqueeze(1).to_broadcast([P, T // 2, V1]), ALU.mult)\
                        .then_inc(y_half, 1)
                with pool.Fori(0, T // NBUF) as g:
                    step.enter(g, 2 * NBUF)
                    for b in range(NBUF):
                        file(h, g, b)
                    step.leave(T // NBUF)
            pool.wait_ge(cand_used, 2 * T)
            pool.wait_ge(rank_ready, 1)
            for t in range(T):
                pool.wait_ge(own_added, t + 1)
                scatter(pool, records, rank_u[:, t:t + 1], rec[:, t, :], sorted_out)
            pool.wait_ge(flag_ready, 1)
            dense = pool.value_load(flag[0:1, 0:1], min_val=0, max_val=1)
            with pool.If(dense):
                dense_pool(pool)
            with pool.Else():
                sparse_pool(pool)

        @block.scalar
        def _(act):
            def weigh(g, b):
                t = g * NBUF + b
                act.activation(xm[b][:], rec[:, t, 0:C], ACT.Copy, scale=mass_sb[:, bass.ds(t, 1)])\
                   .then_inc(xm_ready, 1)

            def count(h, g, b):
                t = g * NBUF + b
                act.wait_ge(adj_landed[b], g * 16 + 16 * (h * (T // NBUF) + 1))
                done = g * NBUF + (h * T + b)
                if h or b or not isinstance(g, int):
                    act.wait_ge(counted, done)
                act.activation(junk[0], adj_buf[b], ACT.Sign, accum_out=n_pos[:, h, bass.ds(t, 1)])
                act.activation(junk[1], adj_buf[b], ACT.Relu, scale=-1.0, accum_out=n_neg[:, h, bass.ds(t, 1)])\
                   .then_inc(counted, 1)

            act.wait_ge(x_loaded, 32)
            for b in range(NBUF):
                weigh(0, b)
            for b in range(NBUF):
                count(0, 0, b)
            act.wait_ge(loaded, 16 * N_CONST)
            act.activation(neg_time[:], time_col[:], ACT.Copy, scale=-1.0).then_inc(neg_ready, 1)
            act.wait_ge(neg_ready, 1)
            act.activation(decay0[:], ev0[:], ACT.Exp, scale=neg_time[:, 0:1]).then_inc(decay_ready, 1)
            act.activation(decay1[:], ev1[:], ACT.Exp, scale=neg_time[:, 1:2]).then_inc(decay_ready, 1)
            act.wait_ge(decay_ready, 2)
            act.wait_ge(x_rest_loaded, 16)
            for h in range(2):
                if h:
                    act.wait_ge(adj_summed, T)
                    for t in range(T // 2):
                        scaled = act.activation(yT[:, t * P:(t + 1) * P], bank[t // 4][:, t % 4 * P:(t % 4 + 1) * P],
                                                ACT.Copy, scale=decay0[:, t:t + 1])
                        if t % 4 == 3:
                            scaled.then_inc(y_scaled, 1)
                with act.Fori(1 - h, T // NBUF) as g:
                    for b in range(NBUF):
                        act.wait_ge(adj_summed, h * T + g * NBUF + (b + 1 - NBUF))
                        weigh(g, b)
                        count(h, g, b)
            for j in range(16):
                act.wait_ge(y_turned[j % 2], j // 2 + 1)
                act.activation(y_rows[:, 4 * j:4 * j + 4, 0:C], bank[j % 2][:].rearrange("p (t c) -> p t c", c=C),
                               ACT.Copy).then_inc(y_copied[j % 2], 1)
            act.wait_ge(cand_used, 2 * T)
            act.wait_ge(counted, 2 * T)
            act.activation(junk[0].rearrange("p (t c) -> p t c", c=NCAND), rec[:, :, AT_VAL:AT_VAL + NCAND],
                           ACT.Sign, accum_out=bad[:, 0:1]).then_inc(candidates_counted, 1)
            act.wait_ge(flag_ready, 1)
            dense = act.value_load(flag[0:1, 0:1], min_val=0, max_val=1)
            with act.If(dense):
                dense_scalar(act)
            with act.Else():
                sparse_scalar(act)

        @block.tensor
        def _(pe):
            def add_block(h, g, b, first, last):
                pe.wait_ge(adj_landed[b], g * 16 + 16 * (h * (T // NBUF) + 1))
                pe.wait_ge(xm_ready, g * NBUF + (h * T + b + 1))
                for k in range(8):
                    if h and first:
                        pe.wait_ge(y_scaled, k + 1)
                    mm = pe.matmul(bank[k][:], xm[b][:], adj_buf[b][:, k * BANK:(k + 1) * BANK],
                                   start=first, stop=last)
                mm.then_inc(adj_summed, 1)

            for h in range(2):
                for b in range(NBUF):
                    add_block(h, 0, b, b == 0, False)
                with pe.Fori(1, T // NBUF - 1) as g:
                    for b in range(NBUF):
                        add_block(h, g, b, False, False)
                for b in range(NBUF):
                    add_block(h, T // NBUF - 1, b, False, b == NBUF - 1)
            def count_before():
                pe.wait_ge(const_ready, N_READY)
                pe.wait_ge(hot_ready, 1)
                pe.wait_ge(y_scaled, 8 + 6)
                for k in range(NCLS * T // BANK):
                    pe.matmul(bank[2 + k][:], tri[:], hot[:, k * BANK:(k + 1) * BANK], start=True, stop=True)
                for k in range(NCLS * T // BANK):
                    mm = pe.matmul(bank[4 + k][:], ones[:], hot[:, k * BANK:(k + 1) * BANK], start=True, stop=True)
                mm.then_inc(before_ready, 1)

            pe.wait_ge(y_half, 1)
            pe.wait_ge(ident_ready, 3)
            for j in range(16):
                if j < 2:
                    pe.wait_ge(y_scaled, 8 + j + 1)
                elif j >= 8:
                    pe.wait_ge(y_scaled, j + 1)
                if j == 8:
                    count_before()
                if j >= 2:
                    pe.wait_ge(y_copied[j % 2], j // 2)
                for i in range(4):
                    tp = pe.transpose(bank[j % 2][:, i * P:(i + 1) * P], yT[:, (4 * j + i) * P:(4 * j + i + 1) * P],
                                      ident[:])
                tp.then_inc(y_turned[j % 2], 1)
            for p in range(2):
                pe.wait_ge(y_copied[p], 8)

            pe.wait_ge(bad_ready, 1)
            pe.matmul(bank[6][0:1, 0:1], bad_bf[:], ones[:, 0:1], start=True, stop=True).then_inc(bad_psum, 1)
            pe.wait_ge(flag_ready, 1)
            dense = pe.value_load(flag[0:1, 0:1], min_val=0, max_val=1)
            with pe.If(dense):
                dense_tensor(pe)
            with pe.Else():
                sparse_tensor(pe)

        @block.vector
        def _(dve):
            step = Steps(dve, dve_step)
            def find(h, g, blocks):
                done = g * NBUF + (h * T + blocks[0])
                in_loop = not isinstance(g, int)
                for block in blocks:
                    dve.wait_ge(adj_landed[block], g * 16 + 16 * (h * (T // NBUF) + 1))
                if h or in_loop:
                    dve.wait_ge(cand_used, done - (NBUF - len(blocks)))
                if in_loop:
                    dve.sem_inc(carried, 1)
                segments = [(block, slice(8 * k, 8 * k + 8), slice(k * SEG, (k + 1) * SEG))
                            for block in blocks for k in range(SEGS)]
                for block, eight, seg in segments:
                    last = dve.max(cand_val[block][:, eight], adj_buf[block][:, seg])
                last.then_inc(cand_max, len(blocks))
                dve.wait_ge(cand_max, done + len(blocks))
                if in_loop:
                    dve.sem_inc(carried, 1)
                for block, eight, seg in segments:
                    last = dve.max_index(cand_col[block][:, eight], cand_val[block][:, eight], adj_buf[block][:, seg])
                    if seg.stop == HALF:
                        last.then_inc(cand_ready, 1)

            for h in range(2):
                if h == 0:
                    for b in range(NBUF):
                        find(0, 0, (b,))
                with dve.Fori(1 - h, T // NBUF) as g:
                    for b in range(0, NBUF, 2):
                        find(h, g, (b, b + 1))
            dve.wait_ge(cand_ready, 2 * T)
            dve.wait_ge(counted, 2 * T)
            dve.wait_ge(const_ready, N_READY)
            step(dve.tensor_tensor(degree[:], n_pos[:, 0, :], n_pos[:, 1, :], ALU.add))
            step(dve.tensor_scalar(clipped[:], degree[:], float(FEWEST), float(MOST), ALU.max, ALU.min))
            dve.tensor_tensor(hot.rearrange("p (k t) -> p k t", k=NCLS), clipped[:].unsqueeze(1).to_broadcast([P, NCLS, T]),
                              cls[:].unsqueeze(2).to_broadcast([P, NCLS, T]), ALU.is_equal).then_inc(hot_ready, 1)
            dve.wait_ge(decay_ready, 2)
            dve.wait_ge(adj_summed, 2 * T)
            for t in range(T // 2, T):
                b, i = (t - T // 2) // 4, t % 4
                scaled = dve.scalar_tensor_tensor(
                    out=yT[:, t * P:(t + 1) * P], in0=bank[b][:, i * P:(i + 1) * P],
                    scalar=decay0[:, t:t + 1], in1=decay1[:], op0=ALU.mult, op1=ALU.mult)
                if i == 3:
                    scaled.then_inc(y_scaled, 1)
            dve.wait_ge(diag_loaded, 16)
            dve.reduce_sum(bad[:, 2:3], degree[:], AX_X)
            dve.tensor_reduce(bad[:, 4:5], n_neg[:], mybir.AxisListType.XY, ALU.max)
            dve.reduce_max(bad[:, 5:6], degree[:], AX_X)
            step(dve.tensor_reduce(bad[:, 6:7], diag[:], AX_X, ALU.min))
            dve.tensor_scalar(bad[:, 4:5], bad[:, 4:5], 0.0, None, ALU.not_equal)
            dve.tensor_scalar(bad[:, 5:6], bad[:, 5:6], float(SLOTS[0] + 1), None, ALU.is_gt)
            step(dve.tensor_scalar(bad[:, 6:7], bad[:, 6:7], 0.0, None, ALU.is_le))
            dve.wait_ge(before_ready, 1)
            dve.wait_ge(hot_ready, 1)
            NB = NCLS * T // BANK
            for k in range(NB):
                step(dve.tensor_tensor_scan(up[:, k * BANK:(k + 1) * BANK], bank[4 + k][:], no_rows[:],
                                            0.0 if k == 0 else up[:, k * BANK - 1:k * BANK], ALU.add, ALU.add))
            for k in range(NB):
                cut = slice(k * BANK, (k + 1) * BANK)
                last = dve.tensor_tensor(place[:, cut], up[:, cut], bank[4 + k][:], ALU.subtract)
            step(last)
            for k in range(NB):
                cut = slice(k * BANK, (k + 1) * BANK)
                last = dve.tensor_tensor(place[:, cut], place[:, cut], bank[2 + k][:], ALU.add)
            step(last)
            step(dve.tensor_tensor(place, place, hot, ALU.mult))
            step(dve.tensor_reduce(rank[:], place.rearrange("p (k t) -> p t k", k=NCLS), AX_X, ALU.add))
            dve.tensor_copy(y_rows[:, :, C], rank[:])
            dve.tensor_copy(rank_u[:], rank[:]).then_inc(rank_ready, 1)
            for p in range(2):
                dve.wait_ge(y_copied[p], 8)
            for t in range(T):
                dve.scalar_tensor_tensor(out=rec[:, t, 0:C], in0=y_rows[:, t, 0:C], scalar=diag[:, t:t + 1],
                                         in1=rec[:, t, 0:C], op0=ALU.mult, op1=ALU.add).then_inc(own_added, 1)
            step(dve.tensor_tensor(bad_cls[:], up.rearrange("p (k t) -> p k t", k=NCLS)[:, :, T - 1], limit[:], ALU.is_gt))
            step(dve.reduce_sum(bad[:, 1:2], bad_cls[:], AX_X))
            dve.wait_ge(candidates_counted, 1)
            step(dve.tensor_tensor(bad[:, 3:4], bad[:, 2:3], bad[:, 0:1], ALU.not_equal))
            step(dve.tensor_tensor(bad[:, 3:4], bad[:, 3:4], bad[:, 1:2], ALU.add))
            step(dve.reduce_sum(bad_sum[:], bad[:, 3:7], AX_X))
            dve.tensor_copy(bad_bf[:], bad_sum[:]).then_inc(bad_ready, 1)
            dve.wait_ge(bad_psum, 1)
            dve.tensor_scalar(flag[:], bank[6][0:1, 0:1], 0.0, None, ALU.is_gt).then_inc(flag_ready, 1)
            dve.wait_ge(flag_ready, 1)
            dense = dve.value_load(flag[0:1, 0:1], min_val=0, max_val=1)
            with dve.If(dense):
                dense_vector(dve, step)
            with dve.Else():
                sparse_vector(dve)


_INS = ["x", "adj", "L0_gnn_mass", "L0_gnn_evals0", "L0_gnn_evals1", "L0_gnn_diffusion_time",
        "L1_gnn_Wq", "L1_gnn_bq", "L1_gnn_bq_row", "L1_gnn_Wk", "L1_gnn_bk", "L1_gnn_bk_row", "L1_gnn_Wv", "L1_gnn_bv",
        "L1_gnn_Ws", "L1_gnn_bs", "L1_gnn_Wb"]


def kernel(**inputs):
    import numpy as _np
    import concourse.bacc as _bacc
    from concourse import mybir as _mybir
    from concourse.bass_utils import run_bass_kernel_spmd as _run

    nc = _bacc.Bacc("TRN2", target_bir_lowering=False, num_devices=1)
    arrays, args = {}, []
    laid_out = {"L0_gnn_mass": (T, P), "L0_gnn_diffusion_time": (2, C), "L1_gnn_bq": (1, C), "L1_gnn_bk": (1, C)}
    for name in _INS:
        a = _np.asarray(inputs[name.removesuffix("_row")])
        if name in laid_out:
            a = a.reshape(laid_out[name]).T
        a = _np.ascontiguousarray(a)
        arrays[f"in_{name}_dram"] = a
        args.append(nc.dram_tensor(f"in_{name}_dram", a.shape, _mybir.dt.from_np(a.dtype), kind="ExternalInput").ap())
    args.append(nc.dram_tensor("out_dram", (N, C), F32, kind="ExternalOutput").ap())
    build_program(nc, *args)
    r = _run(nc, [arrays], core_ids=[0])
    return r.results[0]["out_dram"]
```
